# Optimizing a Trainium2 kernel written in Bass

```python
import numpy as np
import jax
import jax.numpy as jnp

def _softmax(x, axis=-1):
    return jax.nn.softmax(x, axis=axis)

def _gelu(x):
    return jax.nn.gelu(x, approximate=True)

def _silu(x):
    return jax.nn.silu(x)

def _sigmoid(x):
    return jax.nn.sigmoid(x)

def _layernorm(x, axis=-1, eps=1e-05):
    m = jnp.mean(x, axis=axis, keepdims=True)
    v = jnp.var(x, axis=axis, keepdims=True)
    return (x - m) / jnp.sqrt(v + eps)

def _scatter_add(tgt, idx, src, axis=0):
    return tgt.at[idx].add(src)

def _segment_sum(src, seg, n):
    return jax.ops.segment_sum(src, seg, n)
kernel_name = 'mk_metaformer_d1_conv_nchw128_r2_5f89df'

def setup_inputs(seed: int=0):
    np.random.seed(seed)
    _w = jnp.asarray

    def _rec_inputs():
        import jax
        import jax.numpy as jnp
        _gk = jax.random.key(seed)
        x = -0.000125 + 0.9999 * jax.random.normal(jax.random.fold_in(_gk, 1), (4, 64, 128, 128), jnp.float32)
        return x
    x = _rec_inputs()

    def _L0_conv_setup():
        import jax, jax.numpy as jnp
        import numpy as np
        WS = 8
        HEADS = 4

        def _relative_position_index(ws: int) -> np.ndarray:
            coords = np.stack(np.meshgrid(np.arange(ws), np.arange(ws), indexing='ij'))
            cf = coords.reshape(2, -1)
            rel = cf[:, :, None] - cf[:, None, :]
            rel = rel.transpose(1, 2, 0).copy()
            rel[..., 0] += ws - 1
            rel[..., 1] += ws - 1
            rel[..., 0] *= 2 * ws - 1
            return rel.sum(-1).astype(np.int32)
        key = jax.random.key(seed)
        k1, k2, k3, k4, k5 = jax.random.split(key, 5)
        B, C, H, W = (4, 64, 128, 128)
        x = jax.random.normal(k1, (B, C, H, W), dtype=jnp.float32)
        w_qkv = jax.random.normal(k2, (3 * C, C), dtype=jnp.float32) * 0.02
        bias_table = jax.random.normal(k3, ((2 * WS - 1) ** 2, HEADS), dtype=jnp.float32) * 0.02
        w_proj = jax.random.normal(k4, (C, C), dtype=jnp.float32) * 0.02
        b_proj = jax.random.normal(k5, (C,), dtype=jnp.float32) * 0.02
        rel_index = jnp.asarray(_relative_position_index(WS))
        return {'x': x, 'w_qkv': w_qkv, 'bias_table': bias_table, 'w_proj': w_proj, 'b_proj': b_proj, 'rel_index': rel_index}
    _L0_conv_all = _L0_conv_setup()
    _L0_conv_in = {k: v for k, v in _L0_conv_all.items() if k in ('w_qkv', 'bias_table', 'w_proj', 'b_proj', 'rel_index')}
    del _L0_conv_all

    def _L0_ffn_setup():
        import jax, jax.numpy as jnp
        import numpy as np
        B, N, D, C, E, K = (8, 4096, 64, 64, 8, 2)
        key = jax.random.key(seed)
        k0, k1, k2 = jax.random.split(key, 3)
        x = jax.random.normal(k0, (B, N, D), dtype=jnp.float32)
        router_w = jax.random.normal(k1, (D, E), dtype=jnp.float32) * 0.05
        router_b = jnp.zeros((E,), dtype=jnp.float32)
        expert_w = jax.random.normal(k2, (E, D, C), dtype=jnp.float32) * (1.0 / np.sqrt(D))
        expert_b = jnp.zeros((E, C), dtype=jnp.float32)
        return {'x': x, 'router_w': router_w, 'router_b': router_b, 'expert_w': expert_w, 'expert_b': expert_b}
    _L0_ffn_all = _L0_ffn_setup()
    _L0_ffn_in = {k: v for k, v in _L0_ffn_all.items() if k in ('router_w', 'router_b', 'expert_w', 'expert_b')}
    del _L0_ffn_all
    return {'x': x, 'L0_conv_w_qkv': _L0_conv_in['w_qkv'], 'L0_conv_bias_table': _L0_conv_in['bias_table'], 'L0_conv_w_proj': _L0_conv_in['w_proj'], 'L0_conv_b_proj': _L0_conv_in['b_proj'], 'L0_conv_rel_index': _L0_conv_in['rel_index'], 'L0_ffn_router_w': _L0_ffn_in['router_w'], 'L0_ffn_router_b': _L0_ffn_in['router_b'], 'L0_ffn_expert_w': _L0_ffn_in['expert_w'], 'L0_ffn_expert_b': _L0_ffn_in['expert_b']}

def reference(x, L0_conv_w_qkv, L0_conv_bias_table, L0_conv_w_proj, L0_conv_b_proj, L0_conv_rel_index, L0_ffn_router_w, L0_ffn_router_b, L0_ffn_expert_w, L0_ffn_expert_b):
    import jax
    import jax.numpy as jnp

    def _L0_conv_ref(x, w_qkv, bias_table, w_proj, b_proj, rel_index):
        import jax, jax.numpy as jnp
        import numpy as np
        WS = 8
        HEADS = 4

        def _relative_position_index(ws: int) -> np.ndarray:
            coords = np.stack(np.meshgrid(np.arange(ws), np.arange(ws), indexing='ij'))
            cf = coords.reshape(2, -1)
            rel = cf[:, :, None] - cf[:, None, :]
            rel = rel.transpose(1, 2, 0).copy()
            rel[..., 0] += ws - 1
            rel[..., 1] += ws - 1
            rel[..., 0] *= 2 * ws - 1
            return rel.sum(-1).astype(np.int32)
        B, C, H, W = x.shape
        heads, ws = (HEADS, WS)
        hd = C // heads
        scale = hd ** (-0.5)
        nh, nw = (H // ws, W // ws)
        N = ws * ws
        xh = jnp.transpose(x, (0, 2, 3, 1))
        qkv = xh @ w_qkv.T
        qkv = qkv.reshape(B, nh, ws, nw, ws, 3, heads, hd)
        qkv = jnp.transpose(qkv, (5, 0, 1, 3, 6, 2, 4, 7)).reshape(3, B * nh * nw, heads, N, hd)
        q, k, v = (qkv[0], qkv[1], qkv[2])
        bias = bias_table[rel_index.reshape(-1)].reshape(N, N, heads)
        bias = jnp.transpose(bias, (2, 0, 1))
        attn = jnp.einsum('whnd,whmd->whnm', q, k) * scale + bias[None]
        attn = jax.nn.softmax(attn, axis=-1)
        out = jnp.einsum('whnm,whmd->whnd', attn, v)
        out = out.reshape(B, nh, nw, heads, ws, ws, hd)
        out = jnp.transpose(out, (0, 1, 4, 2, 5, 3, 6)).reshape(B, H, W, C)
        out = out @ w_proj.T + b_proj
        return jnp.transpose(out, (0, 3, 1, 2))

    def _L0_ffn_ref(x, router_w, router_b, expert_w, expert_b):
        import jax, jax.numpy as jnp
        import numpy as np
        B, N, D, C, E, K = (8, 4096, 64, 64, 8, 2)
        router_probs = jax.nn.softmax(x @ router_w + router_b, axis=-1)
        top_p, top_i = jax.lax.top_k(router_probs, K)
        top_p = top_p / jnp.sum(top_p, axis=-1, keepdims=True)
        expert_out = jnp.einsum('bnd,edc->bnec', x, expert_w) + expert_b
        gathered = jnp.take_along_axis(expert_out, top_i[..., None], axis=2)
        return jnp.einsum('bnk,bnkc->bnc', top_p, gathered)

    def _gn(v, G=32, eps=1e-05):
        B_, C_, H_, W_ = v.shape
        g = v.reshape(B_, G, C_ // G, H_, W_)
        m = jnp.mean(g, axis=(2, 3, 4), keepdims=True)
        s = jnp.var(g, axis=(2, 3, 4), keepdims=True)
        return ((g - m) / jnp.sqrt(s + eps)).reshape(v.shape)

    def _ln_c(v, eps=1e-06):
        m = jnp.mean(v, axis=1, keepdims=True)
        s = jnp.var(v, axis=1, keepdims=True)
        return (v - m) / jnp.sqrt(s + eps)

    def _ln_t(v, eps=1e-05):
        m = jnp.mean(v, axis=-1, keepdims=True)
        s = jnp.var(v, axis=-1, keepdims=True)
        return (v - m) / jnp.sqrt(s + eps)

    def _to_tokens(v):
        B_, C_, H_, W_ = v.shape
        return v.reshape(B_, C_, H_ * W_).transpose(0, 2, 1)

    def _from_tokens(t, like):
        B_, C_, H_, W_ = like.shape
        return t.transpose(0, 2, 1).reshape(B_, C_, H_, W_)
    x = x + _L0_conv_ref(_ln_c(x), L0_conv_w_qkv, L0_conv_bias_table, L0_conv_w_proj, L0_conv_b_proj, L0_conv_rel_index)
    t = _to_tokens(x)
    t = t + _L0_ffn_ref(_ln_t(t), L0_ffn_router_w, L0_ffn_router_b, L0_ffn_expert_w, L0_ffn_expert_b)
    x = _from_tokens(t, x)
    return x

_drawn_inputs = setup_inputs


def setup_inputs(seed=0):
    import zlib

    import numpy as np

    out = dict(_drawn_inputs(seed))
    spreads = {'L0_ffn_router_b': (0.0, 0.1), 'L0_ffn_expert_b': (0.0, 0.1)}
    factors = {'L0_conv_bias_table': 40.23}
    for name, (base, spread) in spreads.items():
        noise = np.random.default_rng([zlib.crc32(name.encode()), seed]).standard_normal(out[name].shape)
        drawn = base * np.exp(spread * noise) if base else spread * noise
        out[name] = jnp.asarray(drawn.astype(out[name].dtype))
    for name, factor in factors.items():
        out[name] = (out[name] * factor).astype(out[name].dtype)
    return out
```

```python
from contextlib import ExitStack

import concourse.bass as bass
from concourse import mybir

F32 = mybir.dt.float32
BF16 = mybir.dt.bfloat16
I32 = mybir.dt.int32
ALU = mybir.AluOpType
ACT = mybir.ActivationFunctionType
AX_X = mybir.AxisListType.X

P = 128
WS = 8
N = WS * WS
HEADS, HD = 4, 16
C = HEADS * HD
E = 8
PARTS = 3
U = 4
SLOTS = 16
BIG = 3.0e38

CONSTS = {}
_at = 0
for _name, _w in (("centre", P), ("mean", P), ("ident", P), ("head", HEADS), ("pair", 32), ("tile", P),
                  ("order", E), ("row", 2)):
    CONSTS[_name] = (_at, _at + _w)
    _at += _w
NCONST = _at
WQ, WK, WV, WR, WE = 0, P, 2 * P, 3 * P, 3 * P + 32
NWEIGHT = WE + 4 * C


def build_program(nc, x, weights, proj, small, expert_bias, table, rel, consts, select_host, out):
    B, _, H, W = x.shape
    LT = WS * W
    NW = W // WS
    STRIPS = (B // 2) * (H // WS)
    CH = LT // 2
    UNITS = NW // 2
    GROUPS = UNITS // 2
    ITEMS = 16
    x_rows = x.rearrange("b c h w -> (b c) (h w)")
    out_rows = out.rearrange("b c h w -> (b c) (h w)")
    PAIRS = B // 2

    with ExitStack() as ctx:
        def sb(name, shape, dt=F32):
            return ctx.enter_context(nc.sbuf_tensor(name, shape, dt))

        def sem(name):
            return ctx.enter_context(nc.semaphore(name))

        cst = sb("cst", [P, NCONST])
        wcen = sb("wcen", [P, NWEIGHT])
        wproj = sb("wproj", [P, P])
        sml = sb("sml", [P, 4])
        ebraw = sb("ebraw", [P, P])
        ebres = sb("ebres", [P, 2, P])
        eb = sb("eb", [P, PARTS, P], BF16)
        tbraw = sb("tbraw", [P, 2, HEADS])
        tbres = sb("tbres", [P, 2, 2, HEADS])
        tb = sb("tb", [P, 2, PARTS, HEADS], BF16)
        tile_id = sb("tile_id", [P, P], BF16)
        ident_bf = sb("ident_bf", [P, P], BF16)
        select = sb("select", [P, 8, P], BF16)
        bias_hm = sb("bias_hm", [P, HEADS, N], BF16)
        bias_l = sb("bias_l", [P, HEADS, N], BF16)

        xs = [sb(f"xs{b}", [P, LT]) for b in range(4)]
        sq = [sb(f"sq{c}", [P, CH]) for c in range(2)]
        rstd = [sb(f"rstd{c}", [P, CH]) for c in range(2)]
        xr = [sb(f"xr{b}", [P, NW, N]) for b in range(2)]
        qbd = [sb(f"qbd{b}", [P, NW, 2, N]) for b in range(2)]
        kex = [sb(f"kex{b}", [P, NW, HEADS, N]) for b in range(2)]
        vbd = [sb(f"vbd{b}", [P, NW, P]) for b in range(2)]
        mx = [sb(f"mx{b}", [P, 8]) for b in range(2)]
        shifted = [sb(f"shifted{b}", [P, 8, N]) for b in range(2)]
        probs = [sb(f"probs{b}", [P, 2, HEADS * N]) for b in range(2)]
        pt = [sb(f"pt{b}", [P, 4, 2, 2, N]) for b in range(2)]
        lnd = sb("lnd", [P, 256])
        rden = [sb(f"rden{b}", [P, 256]) for b in range(2)]
        onrm = [sb(f"onrm{c}", [P, CH]) for c in range(2)]
        prj = [sb(f"prj{c}", [P, CH]) for c in range(2)]
        tt = [sb(f"tt{b}", [P, LT]) for b in range(4)]
        sq2 = [sb(f"sqb{c}", [P, CH]) for c in range(2)]
        rstd2 = [sb(f"rstdb{c}", [P, CH]) for c in range(2)]
        xn2 = [sb(f"xnb{b}", [P, LT]) for b in range(2)]
        xd = [sb(f"xd{b}", [P, 2, LT]) for b in range(2)]
        lg = sb("lg", [P, CH])
        L = sb("L", [P, 16, E])
        L2 = sb("L2", [P, 16, E])
        eq = sb("eq", [P, 16, E])
        cand = sb("cand", [P, 16, E])
        oh1 = sb("oh1", [P, 16, E])
        oh2 = sb("oh2", [P, 16, E])
        m1 = sb("m1", [P, 16])
        m2 = sb("m2", [P, 16])
        rk = sb("rk", [P, 16])
        dl = sb("dl", [P, 16])
        ed = sb("ed", [P, 16])
        es = sb("es", [P, 16])
        g1 = sb("g1", [P, 16])
        g2 = sb("g2", [P, 16])
        ga = sb("ga", [P, 16, E])
        gb = sb("gb", [P, 16, E])
        gr = sb("gr", [P, 16, E])
        gs = sb("gs", [P, 16, E])
        gp = sb("gp", [P, 8, P // 16, 16], BF16)
        gT = [sb(f"gT{b}", [P, LT], BF16) for b in range(2)]
        z = [sb(f"z{b}", [P, CH]) for b in range(2)]
        ob = [sb(f"ob{b}", [P, LT]) for b in range(2)]

        bank = ctx.enter_context(nc.psum_tensor("bank", [P, 8, 512], F32))
        S_BANK, PT_BANK, OD_BANK, PRE, G_BANK, Y_BANK = (0, 1), 2, 3, 4, (5, 6), 7

        def cv(name, rows=P):
            return cst[0:rows, CONSTS[name][0]:CONSTS[name][1]]

        def windows(t, c):
            v = t[:, :].rearrange("p (r w k) -> p w r k", r=WS, k=WS)
            return v[:, c * (NW // 2):(c + 1) * (NW // 2)]

        def as_windows(ap):
            return ap.rearrange("p (w r k) -> p w r k", r=WS, k=WS)

        def chunk(t, c):
            return t[:, c * (NW // 2):(c + 1) * (NW // 2), :].rearrange("p w n -> p (w n)")

        def dup(ap):
            return ap.unsqueeze(1).broadcast_to([P, 2, ap.shape[1]])

        pre_bf = bank[:, PRE, :].bitcast(BF16)
        wraw = xd[1][:, 0, 0:NWEIGHT]
        select_raw = xd[0][:, 0, :]
        rel_int = kex[0][:, :, :, :].rearrange("p w h n -> p (w h n)").bitcast(I32)
        hot = kex[1][:, :, :, :].rearrange("p w h n -> p (w h n)").bitcast(BF16)
        onehot = [hot[:, half * N * N:(half + 1) * N * N].rearrange("p (k q) -> p k q", q=N) for half in range(2)]

        loaded = sem("loaded")
        setup_dve = sem("setup_dve")
        setup_pe = sem("setup_pe")
        setup_dve_own = sem("setup_dve_own")
        rel_loaded = sem("rel_loaded")
        x_loaded = [sem(f"x_loaded{b}") for b in range(4)]
        xd_loaded = [sem(f"xd_loaded{b}") for b in range(2)]
        stored = [sem(f"stored{b}") for b in range(2)]
        centred, var_full = sem("centred"), sem("var_full")
        sq_ready, ln_done, rstd_ready, xr_ready = sem("sq_ready"), sem("ln_done"), sem("rstd_ready"), sem("xr_ready")
        q_full, k_full, v_full = sem("q_full"), sem("k_full"), sem("v_full")
        q_ready, k_ready, v_ready = sem("q_ready"), sem("k_ready"), sem("v_ready")
        s_full, max_done, shift_done, exp_done = sem("s_full"), sem("max_done"), sem("shift_done"), sem("exp_done")
        t_full, pt_ready, od_full, lnd_done, rden_ready, o_ready = (sem("t_full"), sem("pt_ready"), sem("od_full"),
                                                                  sem("lnd_done"), sem("rden_ready"), sem("o_ready"))
        prj_full, prj_ready, t_ready = sem("prj_full"), sem("prj_ready"), sem("t_ready")
        centred2, var2_full = sem("centred2"), sem("var2_full")
        sq2_ready, ln2_done, rstd2_ready, xn2_ready = (sem("sq2_ready"), sem("ln2_done"), sem("rstd2_ready"),
                                                       sem("xn2_ready"))
        lg_full, lg_ready, lgt_full, L_ready = sem("lg_full"), sem("lg_ready"), sem("lgt_full"), sem("L_ready")
        top, delta_ready, ed_ready, g_ready = sem("top"), sem("delta_ready"), sem("ed_ready"), sem("g_ready")
        gate, gp_ready, gt_full, gt_ready = sem("gate"), sem("gp_ready"), sem("gt_full"), sem("gt_ready")
        g_full, z_ready, e_done, y_ready = sem("g_full"), sem("z_ready"), sem("e_done"), sem("y_ready")

        TOP = 12
        GATE = 6

        ROUNDS = [("gT", -2, gt_ready, 1, 1), ("C0", 1, sq_ready, 2, 1), ("C1", 1, sq_ready, 2, 2),
                  ("var0", 1, ln_done, 2, 1), ("var1", 1, ln_done, 2, 2), ("proj1", -1, prj_ready, 2, 2),
                  ("D0", -1, sq2_ready, 2, 1), ("D1", -1, sq2_ready, 2, 2),
                  ("war0", -1, ln2_done, 2, 1), ("Q0", 1, q_ready, 4, 2), ("war1", -1, ln2_done, 2, 2),
                  ("K0", 1, k_ready, 2, 1), ("Q1", 1, q_ready, 4, 4), ("K1", 1, k_ready, 2, 2),
                  ("V0", 1, v_ready, 4, 1), ("V1", 1, v_ready, 4, 2), ("proj0", 0, prj_ready, 2, 1),
                  ("V2", 1, v_ready, 4, 3), ("router", -1, lg_ready, 1, 1), ("V3", 1, v_ready, 4, 4),
                  ("lgT", -1, L_ready, 1, 1)]
        NAMES = [r[0] for r in ROUNDS]

        class Step:

            def __init__(self, c, n, inner):
                self.c, self.n, self.inner = c, n, inner

            def strip(self, off):
                return Strip(self.c + off, self.n, self.inner)

        class Strip:

            def __init__(self, c, n, inner):
                self.c, self.n, self.inner = c, n, inner
                self.on = inner or 0 <= c < STRIPS

            def buf(self, k):
                return self.c % k

            def count(self, per, k, lag=0):
                v = per * (self.c - lag) + k
                return v + per * U * self.n if self.inner else v

            def rounds(self, k, of):
                v = of * (self.c // k)
                return v + of * (U // k) * self.n if self.inner else v

        def wait(eng, s, value):
            if isinstance(value, int) and value <= 0:
                return
            eng.wait_ge(s, value)

        def steps(run):
            first, last = -1, STRIPS + 1
            lo = 6
            n = (STRIPS - 1 - lo) // U
            for i in range(first, lo):
                run(Step(i, 0, False))
            with nc.Fori(0, n, engines=(run.engine,)) as r:
                for v in range(U):
                    run(Step(lo + v, r, True))
            for i in range(lo + n * U, last + 1):
                run(Step(i, 0, False))

        def stepped(engine_type):
            def mark(f):
                class Run:
                    engine = engine_type

                    def __call__(self, st):
                        f(st)
                steps(Run())
            return mark

        block = ctx.enter_context(nc.Block())
        ET = mybir.EngineType

        @block.sync
        def _(sp):
            for dst, src in ((cst[:, :], consts), (wraw, weights), (wproj[:, :], proj), (sml[:, :], small),
                             (ebraw[:, :], expert_bias), (select_raw, select_host)):
                sp.dma_start(dst, src).then_inc(loaded, 16)
            sp.dma_start(tbraw[:, :, :].rearrange("p a h -> p (a h)"), table).then_inc(loaded, 16)
            sp.dma_start(rel_int, rel.rearrange("k q -> (k q)").partition_broadcast(P)).then_inc(rel_loaded, 16)

            def place(rows, strip):
                pr = strip.buf(PAIRS)
                return rows[pr * P:(pr + 1) * P, bass.ds(strip.rounds(PAIRS, LT), LT)]

            def load(strip):
                src = place(x_rows, strip)
                used = strip.count(2, 2, lag=4)
                wait(sp, t_ready, used)
                sp.dma_start(xs[strip.buf(4)][:, :], src).then_inc(x_loaded[strip.buf(4)], 16)

            load(Strip(0, 0, False))

            @stepped(ET.SP)
            def _(st):
                nx = st.strip(2)
                if nx.on:
                    load(nx)
                r = st.strip(-1)
                if r.on:
                    wait(sp, xn2_ready, r.count(2, 2))
                    for a in range(2):
                        for d in range(2):
                            sp.dma_start(xd[r.buf(2)][64 * d:64 * d + 64, a, :],
                                         xn2[r.buf(2)][64 * a:64 * a + 64, :]).then_inc(xd_loaded[r.buf(2)], 16)
                m = st.strip(-2)
                if m.on:
                    dst, summed = place(out_rows, m), m.count(2, 2)
                    wait(sp, y_ready, summed)
                    sp.dma_start(dst, ob[m.buf(2)][:, :]).then_inc(stored[m.buf(2)], 16)

            for b in range(2):
                sp.wait_ge(stored[b], 16 * (STRIPS // 2))

        @block.tensor
        def _(pe):
            mm = nc.tensor.matmul
            pe.wait_ge(loaded, 112)
            mm(bank[:, 0, 0:WR], cv("centre"), wraw[:, 0:WR], start=True, stop=True)
            mm(bank[:, 1, 0:NWEIGHT - WR], cv("centre"), wraw[:, WR:NWEIGHT], start=True, stop=True).then_inc(setup_pe, 1)
            pe.wait_ge(setup_dve, 5)
            for k in range(N):
                for q in (0, N):
                    dst = bank[q:q + N, 2 + k // 32, 12 * (k % 32):12 * (k % 32) + 12]
                    for half in range(2):
                        last = mm(dst, onehot[half][:, k, :], tb[:, half, :, :].rearrange("p s h -> p (s h)"),
                                  start=(half == 0), stop=(half == 1), skip_group_check=True)
            last.then_inc(setup_pe, 1)
            pe.wait_ge(setup_dve, 7)

            def pre_free(st, name):
                at, c = NAMES.index(name), st.c
                while True:
                    at -= 1
                    if at < 0:
                        at, c = len(ROUNDS) - 1, c - 1
                    if c < -1:
                        return
                    _, off, s, per, k = ROUNDS[at]
                    if st.inner or 0 <= c + off < STRIPS:
                        wait(pe, s, Strip(c + off, st.n, st.inner).count(per, k))
                        return

            def scores(st, u):
                s = st.strip(0)
                b = bank[:, S_BANK[u % 2], :]
                if u % 4 == 0:
                    pe.wait_ge(q_ready, s.count(4, 2 * (u // 4) + 2))
                    pe.wait_ge(k_ready, s.count(2, u // 4 + 1))
                wait(pe, shift_done, s.count(UNITS, u - 1))
                bh = bias_hm[:, :, :].rearrange("p h k -> p (h k)")
                bl = bias_l[:, :, :].rearrange("p h k -> p (h k)")
                mm(b, tile_id[:, :], dup(bh), start=True, stop=False, skip_group_check=True)
                mm(b, tile_id[:, :], dup(bl), start=False, stop=False, skip_group_check=True)
                for j in range(2):
                    w = 2 * u + j
                    last = mm(b[:, 256 * j:256 * j + 256], qbd[s.buf(2)][:, w, :, :].rearrange("p a q -> p (a q)"),
                              kex[s.buf(2)][:, w, :, :].rearrange("p h k -> p (h k)"), start=False, stop=(j == 1),
                              skip_group_check=True)
                last.then_inc(s_full, 1)

            def transposes(s, u):
                pe.wait_ge(exp_done, s.count(UNITS, u + 1))
                wait(pe, pt_ready, s.count(UNITS, u))
                for j in range(4):
                    last = nc.tensor.transpose(bank[:, PT_BANK, 128 * j:128 * j + 128],
                                               probs[u % 2][:, j // 2, 128 * (j % 2):128 * (j % 2) + 128], cv("ident"))
                last.then_inc(t_full, 1)

            def values(s, u):
                g = u // 2
                pe.wait_ge(pt_ready, s.count(UNITS, u + 1))
                if u % 2 == 0:
                    pe.wait_ge(v_ready, s.count(4, g + 1))
                    wait(pe, o_ready, s.count(GROUPS, g))
                for wl in range(2):
                    w4 = 2 * (u % 2) + wl
                    for a in range(2):
                        for j in range(2):
                            q = 64 * a + 32 * j
                            last = mm(bank[q:q + 32, OD_BANK, N * w4:N * w4 + N], vbd[s.buf(2)][:, 2 * u + wl, q:q + 32],
                                      pt[g % 2][:, w4, j, a, :], start=True, stop=True, skip_group_check=True)
                if u % 2 == 1:
                    for a in range(2):
                        for j in range(2):
                            q = 64 * a + 32 * j
                            last = mm(bank[q:q + 32, OD_BANK, 256:512], cv("pair"), pt[g % 2][:, :, j, a, :],
                                      start=True, stop=True, skip_group_check=True)
                    last.then_inc(od_full, 1)

            def project(st, s, c, name):
                pe.wait_ge(o_ready, s.count(GROUPS, 2 * c + 2))
                pre_free(st, name)
                mm(bank[:, PRE, :], wproj[:, :], onrm[c][:, :], start=True, stop=True).then_inc(prj_full, 1)

            def gates_wide(s, n):
                c, j, a = n // 8, n % 8 // 2, n % 2
                if n == 0:
                    pe.wait_ge(gt_ready, s.count(1, 1))
                wait(pe, z_ready, s.count(ITEMS, n - 1))
                mm(bank[:, G_BANK[n % 2], :], select[:, 4 * a + j, :], gT[s.buf(2)][:, c * CH:(c + 1) * CH],
                   start=True, stop=True).then_inc(g_full, 1)

            def experts(s, n):
                c, j, a = n // 8, n % 8 // 2, n % 2
                if n % 8 == 0:
                    wait(pe, y_ready, s.count(2, c))
                    for k in range(PARTS):
                        mm(bank[:, Y_BANK, :], eb[:, k, :], gT[s.buf(2)][:, c * CH:(c + 1) * CH],
                           start=(k == 0), stop=False, skip_group_check=True)
                pe.wait_ge(z_ready, s.count(ITEMS, n + 1))
                mm(bank[64 * a:64 * a + 64, Y_BANK, :], wcen[:, WE + C * j:WE + C * j + C], z[n % 2][:, :],
                   start=False, stop=(j == 3), skip_group_check=True).then_inc(e_done, 1)

            @stepped(ET.PE)
            def _(st):
                pre, att, old, moe = st.strip(1), st.strip(0), st.strip(-1), st.strip(-2)
                for k in range(SLOTS):
                    if k == 0 and moe.on:
                        pe.wait_ge(gp_ready, moe.count(1, 1))
                        pre_free(st, "gT")
                        for t8 in range(8):
                            ttl, c = t8 // 2, t8 % 2
                            last = nc.tensor.transpose(pre_bf[:, c * CH + 128 * ttl:c * CH + 128 * ttl + 128],
                                                       gp[:, t8, :, :].rearrange("p s e -> p (s e)"), ident_bf[:, :])
                        last.then_inc(gt_full, 1)
                    if k % 2 == 0 and att.on:
                        scores(st, k // 2)
                    if pre.on:
                        if k in (0, 1):
                            if k == 0:
                                pe.wait_ge(x_loaded[pre.buf(4)], pre.rounds(4, 16) + 16)
                            pre_free(st, f"C{k}")
                            mm(bank[:, PRE, :], cv("centre"), windows(xs[pre.buf(4)], k), start=True,
                               stop=True).then_inc(centred, 1)
                        if k in (2, 3):
                            pe.wait_ge(sq_ready, pre.count(2, k - 1))
                            pre_free(st, f"var{k - 2}")
                            mm(bank[:, PRE, :], cv("mean"), sq[k - 2][:, :], start=True, stop=True).then_inc(var_full, 1)
                    if k == 0 and old.on:
                        transposes(old, 7)
                    if k == 1 and old.on:
                        values(old, 7)
                    if k == 3 and old.on:
                        project(st, old, 1, "proj1")
                    if k in (4, 5) and old.on:
                        pe.wait_ge(t_ready, old.count(2, k - 3))
                        pre_free(st, f"D{k - 4}")
                        mm(bank[:, PRE, :], cv("centre"), tt[old.buf(4)][:, (k - 4) * CH:(k - 3) * CH], start=True,
                           stop=True).then_inc(centred2, 1)
                    if k in (6, 7) and old.on:
                        pe.wait_ge(sq2_ready, old.count(2, k - 5))
                        pre_free(st, f"war{k - 6}")
                        mm(bank[:, PRE, :], cv("mean"), sq2[k - 6][:, :], start=True, stop=True).then_inc(var2_full, 1)
                    if k in (6, 8) and pre.on:
                        c = (k - 6) // 2
                        pe.wait_ge(xr_ready, pre.count(2, c + 1))
                        pre_free(st, f"Q{c}")
                        mm(bank[:, PRE, :], wcen[:, WQ:WQ + P], chunk(xr[pre.buf(2)], c), start=True,
                           stop=True).then_inc(q_full, 1)
                    if k in (7, 9) and pre.on:
                        c = (k - 7) // 2
                        pre_free(st, f"K{c}")
                        mm(bank[:, PRE, :], wcen[:, WK:WK + P], chunk(xr[pre.buf(2)], c), start=True,
                           stop=True).then_inc(k_full, 1)
                    if k in (10, 11, 12, 13) and pre.on:
                        g = k - 10
                        pre_free(st, f"V{g}")
                        for wl in range(4):
                            for q in (0, N):
                                last = mm(bank[q:q + N, PRE, 128 * wl:128 * wl + 128], xr[pre.buf(2)][:, 4 * g + wl, :],
                                          wcen[:, WV:WV + P], start=True, stop=True)
                        last.then_inc(v_full, 1)
                    if k == 11 and att.on:
                        project(st, att, 0, "proj0")
                    if k == 12 and old.on:
                        pe.wait_ge(xn2_ready, old.count(2, 2))
                        pre_free(st, "router")
                        for c in range(2):
                            last = mm(bank[32 * c:32 * c + 32, PRE, :], wcen[:, WR:WR + 32],
                                      xn2[old.buf(2)][:, c * CH:(c + 1) * CH], start=True, stop=True)
                        last.then_inc(lg_full, 1)
                    if k == 14 and old.on:
                        pe.wait_ge(lg_ready, old.count(1, 1))
                        pre_free(st, "lgT")
                        for ttl in range(4):
                            last = nc.tensor.transpose(bank[:, PRE, 128 * ttl:128 * ttl + 128],
                                                       lg[:, 128 * ttl:128 * ttl + 128], cv("ident"))
                        last.then_inc(lgt_full, 1)
                    if att.on:
                        if k % 2 == 0 and k >= 2:
                            transposes(att, k // 2 - 1)
                        if k % 2 == 1 and k >= 3:
                            values(att, (k - 3) // 2)
                    if moe.on:
                        gates_wide(moe, k)
                        if k:
                            experts(moe, k - 1)
                        if k == SLOTS - 1:
                            experts(moe, k)

        @block.scalar
        def _(act):
            af = nc.scalar.activation
            act.wait_ge(loaded, 112)

            def exps(s, u):
                act.wait_ge(shift_done, s.count(UNITS, u + 1))
                wait(act, t_full, s.count(UNITS, u - 1))
                af(probs[u % 2][:, :, :].rearrange("p w k -> p (w k)"),
                   shifted[u % 2][:, :, :].rearrange("p g k -> p (g k)"), ACT.Exp).then_inc(exp_done, 1)

            def move_pt(s, u):
                g = u // 2
                act.wait_ge(t_full, s.count(UNITS, u + 1))
                if u % 2 == 0:
                    wait(act, od_full, s.count(GROUPS, g - 1))
                af(pt[g % 2][:, 2 * (u % 2):2 * (u % 2) + 2, :, :, :].rearrange("p w j a q -> p (w j a q)"),
                   bank[:, PT_BANK, :], ACT.Copy).then_inc(pt_ready, 1)

            def inverse_sums(s, g):
                act.wait_ge(od_full, s.count(GROUPS, g + 1))
                wait(act, rden_ready, s.count(GROUPS, g))
                af(lnd[:, :], bank[:, OD_BANK, 256:512], ACT.Ln).then_inc(lnd_done, 1)
                act.wait_ge(lnd_done, s.count(GROUPS, g + 1))
                wait(act, o_ready, s.count(GROUPS, g - 1))
                af(rden[g % 2][:, :], lnd[:, :], ACT.Exp, scale=-1.0).then_inc(rden_ready, 1)

            def square(s, full, ready, used, dst, c):
                act.wait_ge(full, s.count(2, c + 1))
                wait(act, used, s.count(2, c + 1, lag=1))
                af(dst[c][:, :], bank[:, PRE, :], ACT.Square).then_inc(ready, 1)

            def inverse_std(s, full, ln, ready, used, tmp, dst, eps, c):
                act.wait_ge(full, s.count(2, c + 1))
                af(tmp[c][:, :], bank[:, PRE, :], ACT.Ln, bias=sml[:, eps:eps + 1]).then_inc(ln, 1)
                act.wait_ge(ln, s.count(2, c + 1))
                wait(act, used, s.count(2, c + 1, lag=1))
                af(dst[c][:, :], tmp[c][:, :], ACT.Exp, scale=-0.5).then_inc(ready, 1)

            def move_proj(s, c):
                act.wait_ge(prj_full, s.count(2, c + 1))
                wait(act, t_ready, s.count(2, c + 1, lag=1))
                af(prj[c][:, :], bank[:, PRE, :], ACT.Identity, bias=sml[:, 0:1]).then_inc(prj_ready, 1)

            @stepped(ET.Activation)
            def _(st):
                pre, att, old = st.strip(1), st.strip(0), st.strip(-1)
                for k in range(SLOTS):
                    if k in (0, 1) and pre.on:
                        square(pre, centred, sq_ready, rstd_ready, sq, k)
                    if k == 0 and old.on:
                        exps(old, 7)
                        move_pt(old, 7)
                    if k == 1 and old.on:
                        inverse_sums(old, 3)
                    if k in (2, 3) and pre.on:
                        inverse_std(pre, var_full, ln_done, rstd_ready, xr_ready, sq, rstd, 2, k - 2)
                    if k == 3 and old.on:
                        move_proj(old, 1)
                    if k in (4, 5) and old.on:
                        square(old, centred2, sq2_ready, rstd2_ready, sq2, k - 4)
                    if k in (6, 7) and old.on:
                        inverse_std(old, var2_full, ln2_done, rstd2_ready, xn2_ready, sq2, rstd2, 3, k - 6)
                    if k in (6, 8) and pre.on:
                        c = (k - 6) // 2
                        act.wait_ge(q_full, pre.count(2, c + 1))
                        wait(act, s_full, pre.count(UNITS, UNITS, lag=2))
                        for a in range(2):
                            af(qbd[pre.buf(2)][64 * a:64 * a + 64, 8 * c:8 * c + 8, a, :],
                               bank[64 * a:64 * a + 64, PRE, :].rearrange("p (w q) -> p w q", q=N), ACT.Copy,
                               scale=float(HD) ** -0.5).then_inc(q_ready, 1)
                    if k == 11 and att.on:
                        move_proj(att, 0)
                    if k == 12 and old.on:
                        act.wait_ge(lg_full, old.count(1, 1))
                        wait(act, lgt_full, old.count(1, 1, lag=1))
                        af(lg[0:64, :], bank[0:64, PRE, :], ACT.Identity, bias=sml[0:64, 1:2]).then_inc(lg_ready, 1)
                    if k == 15 and old.on:
                        act.wait_ge(delta_ready, old.count(1, 1))
                        af(ed[:, :], dl[:, :], ACT.Exp).then_inc(ed_ready, 1)
                    if att.on:
                        if k % 2 == 0 and k >= 2:
                            exps(att, k // 2 - 1)
                            move_pt(att, k // 2 - 1)
                        if k % 4 == 1 and k >= 5:
                            inverse_sums(att, (k - 5) // 4)

        @block.gpsimd
        def _(pool):
            tt_ = nc.gpsimd.tensor_tensor
            for b in range(2):
                nc.gpsimd.memset(qbd[b][:, :, :, :], 0.0).then_inc(setup_dve, 1)

            @stepped(ET.Pool)
            def _(st):
                pre, att, old, moe = st.strip(1), st.strip(0), st.strip(-1), st.strip(-2)

                def residual(s, c):
                    pool.wait_ge(prj_ready, s.count(2, c + 1))
                    wait(pool, y_ready, s.count(2, c + 1, lag=4))
                    tt_(as_windows(tt[s.buf(4)][:, c * CH:(c + 1) * CH]), as_windows(prj[c][:, :]),
                        windows(xs[s.buf(4)], c), op=ALU.add).then_inc(t_ready, 1)

                if old.on:
                    residual(old, 1)
                if pre.on:
                    for c in range(2):
                        pool.wait_ge(rstd_ready, pre.count(2, c + 1))
                        if c == 0:
                            pool.wait_ge(x_loaded[pre.buf(4)], pre.rounds(4, 16) + 16)
                        wait(pool, v_ready, pre.count(4, 4, lag=2))
                        tt_(as_windows(chunk(xr[pre.buf(2)], c)), windows(xs[pre.buf(4)], c),
                            as_windows(rstd[c][:, :]), op=ALU.mult).then_inc(xr_ready, 1)
                if old.on:
                    for c in range(2):
                        pool.wait_ge(rstd2_ready, old.count(2, c + 1))
                        wait(pool, lg_full, old.count(1, 1, lag=2))
                        wait(pool, xd_loaded[old.buf(2)], old.rounds(2, 64))
                        wait(pool, z_ready, old.count(ITEMS, ITEMS, lag=2))
                        tt_(xn2[old.buf(2)][:, c * CH:(c + 1) * CH], tt[old.buf(4)][:, c * CH:(c + 1) * CH],
                            rstd2[c][:, :], op=ALU.mult).then_inc(xn2_ready, 1)
                if att.on:
                    residual(att, 0)
                if old.on:
                    pool.wait_ge(g_ready, old.count(2, 2))
                    wide = lambda ap: ap.unsqueeze(2).broadcast_to([P, 16, E])
                    part = lambda n: gp[:, :, n, :].rearrange("p t (a e) -> p t a e", a=2)
                    v4 = lambda t: t[:, :, :].rearrange("p (t a) e -> p t a e", a=2)
                    wait(pool, gt_full, old.count(1, 1, lag=1))
                    tt_(ga[:, :, :], oh1[:, :, :], wide(g1[:, :]), op=ALU.mult).then_inc(gate, 1)
                    tt_(gb[:, :, :], oh2[:, :, :], wide(g2[:, :]), op=ALU.mult).then_inc(gate, 1)
                    pool.wait_ge(gate, old.count(GATE, 2))
                    tt_(gr[:, :, :], ga[:, :, :], gb[:, :, :], op=ALU.add).then_inc(gate, 1)
                    tt_(part(0), v4(ga), v4(gb), op=ALU.add).then_inc(gate, 1)
                    pool.wait_ge(gate, old.count(GATE, 4))
                    tt_(v4(gs), v4(gr), part(0), op=ALU.subtract).then_inc(gate, 1)
                    tt_(part(1), v4(gr), part(0), op=ALU.subtract).then_inc(gate, 1)
                    pool.wait_ge(gate, old.count(GATE, 6))
                    tt_(part(2), v4(gs), part(1), op=ALU.subtract).then_inc(gp_ready, 1)

        @block.vector
        def _(dve):
            tt_, red = nc.vector.tensor_tensor, nc.vector.tensor_reduce
            copy = nc.vector.tensor_copy
            dve.wait_ge(loaded, 112)
            dve.wait_ge(setup_pe, 1)
            dve.wait_ge(setup_dve, 2)
            copy(wcen[:, 0:WR], bank[:, 0, 0:WR])
            copy(wcen[:, WR:NWEIGHT], bank[:, 1, 0:NWEIGHT - WR])
            copy(tile_id[:, :], cv("tile"))
            copy(ident_bf[:, :], cv("ident"))
            copy(select[:, :, :].rearrange("p s n -> p (s n)"), select_raw)
            nc.vector.memset(bias_l[:, :, :], 0.0)
            nc.vector.memset(gp[:, :, :, :], 0.0)
            nc.vector.memset(lg[:, :], 0.0)

            def link(ins, n):
                ins.then_inc(setup_dve_own, 1)
                dve.wait_ge(setup_dve_own, n)

            link(copy(eb[:, 0, :], ebraw[:, :]), 1)
            link(tt_(ebres[:, 0, :], ebraw[:, :], eb[:, 0, :], op=ALU.subtract), 2)
            link(copy(eb[:, 1, :], ebres[:, 0, :]), 3)
            link(tt_(eb[:, 2, :], ebres[:, 0, :], eb[:, 1, :], op=ALU.subtract), 4)
            link(copy(tb[:, :, 0, :], tbraw[:, :, :]), 5)
            link(tt_(tbres[:, 0, :, :], tbraw[:, :, :], tb[:, :, 0, :], op=ALU.subtract), 6)
            link(copy(tb[:, :, 1, :], tbres[:, 0, :, :]), 7)
            tt_(tb[:, :, 2, :], tbres[:, 0, :, :], tb[:, :, 1, :], op=ALU.subtract).then_inc(setup_dve, 1)
            dve.wait_ge(rel_loaded, 16)
            for half in range(2):
                nc.vector.tensor_scalar(onehot[half].rearrange("p k q -> p (k q)"), rel_int,
                                        cv("row")[:, half:half + 1], None, ALU.is_equal).then_inc(setup_dve, 1)
            dve.wait_ge(setup_pe, 2)
            for kh in range(2):
                src = bank[:, 2 + kh, 0:384].rearrange("p (k s h) -> p s h k", s=PARTS, h=HEADS)
                for dst, rows, part in ((bias_hm, 0, 0), (bias_hm, 64, 1), (bias_l, 0, 2)):
                    last = copy(dst[rows:rows + 64, :, 32 * kh:32 * kh + 32], src[rows:rows + 64, part, :, :])
                last.then_inc(setup_dve, 1)

            def softmax_shift(s, u):
                b = bank[:, S_BANK[u % 2], :].rearrange("p (g k) -> p g k", k=N)
                dve.wait_ge(s_full, s.count(UNITS, u + 1))
                red(mx[u % 2][:, :], b, axis=AX_X, op=ALU.max).then_inc(max_done, 1)
                dve.wait_ge(max_done, s.count(UNITS, u + 1))
                wait(dve, exp_done, s.count(UNITS, u - 1))
                tt_(shifted[u % 2][:, :, :], b, mx[u % 2][:, :].unsqueeze(2).broadcast_to([P, 8, N]),
                    op=ALU.subtract).then_inc(shift_done, 1)

            def normalise(s, g):
                dve.wait_ge(rden_ready, s.count(GROUPS, g + 1))
                c = g // 2
                wait(dve, prj_full, s.count(2, c + 1, lag=1))
                tt_(onrm[c][:, 256 * (g % 2):256 * (g % 2) + 256], bank[:, OD_BANK, 0:256], rden[g % 2][:, :],
                    op=ALU.mult).then_inc(o_ready, 1)

            def gated(s, n):
                c, a = n // 8, n % 2
                dve.wait_ge(g_full, s.count(ITEMS, n + 1))
                if n == 0:
                    dve.wait_ge(xd_loaded[s.buf(2)], s.rounds(2, 64) + 64)
                wait(dve, e_done, s.count(ITEMS, n - 1))
                tt_(z[n % 2][:, :], bank[:, G_BANK[n % 2], :], xd[s.buf(2)][:, a, c * CH:(c + 1) * CH],
                    op=ALU.mult).then_inc(z_ready, 1)

            def finish(s, c):
                dve.wait_ge(e_done, s.count(ITEMS, 8 * c + 8))
                if c == 0:
                    wait(dve, stored[s.buf(2)], s.rounds(2, 16))
                tt_(windows(ob[s.buf(2)], c), as_windows(bank[:, Y_BANK, :]),
                    as_windows(tt[s.buf(4)][:, c * CH:(c + 1) * CH]), op=ALU.add).then_inc(y_ready, 1)

            def top_two(s):
                n = [0]

                def step(ins):
                    n[0] += 1
                    ins.then_inc(top, 1)
                    dve.wait_ge(top, s.count(TOP, n[0]))

                wide = lambda ap: ap.unsqueeze(2).broadcast_to([P, 16, E])
                order = cv("order").unsqueeze(1).broadcast_to([P, 16, E])

                def pick(vals, m, oh):
                    step(red(m[:, :], vals[:, :, :], axis=AX_X, op=ALU.max))
                    step(tt_(eq[:, :, :], vals[:, :, :], wide(m[:, :]), op=ALU.is_equal))
                    step(tt_(cand[:, :, :], eq[:, :, :], order, op=ALU.mult))
                    step(red(rk[:, :], cand[:, :, :], axis=AX_X, op=ALU.max))
                    step(tt_(oh[:, :, :], cand[:, :, :], wide(rk[:, :]), op=ALU.is_equal))

                wait(dve, gp_ready, s.count(1, 1, lag=1))
                pick(L, m1, oh1)
                step(nc.vector.scalar_tensor_tensor(out=L2[:, :, :], in0=oh1[:, :, :], scalar=-BIG, in1=L[:, :, :],
                                                    op0=ALU.mult, op1=ALU.add))
                pick(L2, m2, oh2)
                tt_(dl[:, :], m2[:, :], m1[:, :], op=ALU.subtract).then_inc(delta_ready, 1)
                dve.wait_ge(ed_ready, s.count(1, 1))
                step(nc.vector.tensor_scalar(es[:, :], ed[:, :], 1.0, None, ALU.add))
                nc.vector.reciprocal(g1[:, :], es[:, :]).then_inc(g_ready, 1)
                dve.wait_ge(g_ready, s.count(2, 1))
                tt_(g2[:, :], ed[:, :], g1[:, :], op=ALU.mult).then_inc(g_ready, 1)
                assert n[0] == TOP

            @stepped(ET.DVE)
            def _(st):
                pre, att, old, moe = st.strip(1), st.strip(0), st.strip(-1), st.strip(-2)
                for k in range(SLOTS):
                    if k == 0 and moe.on:
                        dve.wait_ge(gt_full, moe.count(1, 1))
                        copy(gT[moe.buf(2)][:, :], pre_bf[:, :]).then_inc(gt_ready, 1)
                    if k % 2 == 0 and att.on:
                        softmax_shift(att, k // 2)
                    if k == 1 and old.on:
                        normalise(old, 3)
                    if k in (7, 9) and pre.on:
                        c = (k - 7) // 2
                        dve.wait_ge(k_full, pre.count(2, c + 1))
                        wait(dve, s_full, pre.count(UNITS, UNITS, lag=2))
                        src = bank[:, PRE, :].rearrange("p (w n) -> p w n", n=N)
                        for h in range(0, HEADS):
                            last = nc.vector.tensor_scalar(kex[pre.buf(2)][:, 8 * c:8 * c + 8, h, :], src,
                                                           cv("head")[:, h:h + 1], None, ALU.mult)
                        last.then_inc(k_ready, 1)
                    if k in (10, 11, 12, 13) and pre.on:
                        g = k - 10
                        dve.wait_ge(v_full, pre.count(4, g + 1))
                        wait(dve, od_full, pre.count(GROUPS, GROUPS, lag=2))
                        tt_(vbd[pre.buf(2)][:, 4 * g:4 * g + 4, :].rearrange("p w (m d) -> p (w m) d", d=32),
                            bank[:, PRE, :].rearrange("p (m d) -> p m d", d=32),
                            cv("pair").unsqueeze(1).broadcast_to([P, 16, 32]), op=ALU.mult).then_inc(v_ready, 1)
                    if k == 14 and old.on:
                        dve.wait_ge(lgt_full, old.count(1, 1))
                        copy(L[:, :, :].rearrange("p (t c a) e -> p t c (a e)", a=2, c=2),
                             bank[:, PRE, :].rearrange("p (t c m) -> p t c m", t=4, m=32)[:, :, 0:2, 0:16]).then_inc(L_ready, 1)
                        dve.wait_ge(L_ready, old.count(1, 1))
                    if k % 4 == 1 and k >= 5 and att.on:
                        normalise(att, (k - 5) // 4)
                    if moe.on:
                        gated(moe, k)
                        if k == 8:
                            finish(moe, 0)
                    if k == 15 and old.on:
                        top_two(old)
                    if k == 15 and moe.on:
                        finish(moe, 1)


def constants(np):
    p = np.arange(P)
    a, ch = p // C, p % C
    same = a[:, None] == a[None, :]
    parts = {
        "centre": np.eye(P) - same / C,
        "mean": same / C,
        "ident": np.eye(P),
        "head": ch[:, None] // HD == np.arange(HEADS)[None, :],
        "pair": p[:, None] // N == np.arange(32)[None, :] // HD,
        "tile": p[:, None] % N == p[None, :] % N,
        "order": np.broadcast_to(np.arange(E, 0, -1), (P, E)),
        "row": p[:, None] + P * np.arange(2)[None, :],
    }
    c = np.zeros((P, NCONST), np.float32)
    for name, (lo, hi) in CONSTS.items():
        c[:, lo:hi] = parts[name]
    return c


def select_matrix(np):
    p = np.arange(P)
    cols = np.arange(8 * P)
    img, pair, e2 = cols // (4 * P), cols // P % 4, cols % P // C
    return ((p[:, None] % 16 == (8 * img + 2 * pair + e2)[None, :]) & (p[:, None] < 16 * PARTS)).astype(np.float32)


def kernel(x, L0_conv_w_qkv, L0_conv_bias_table, L0_conv_w_proj, L0_conv_b_proj, L0_conv_rel_index,
           L0_ffn_router_w, L0_ffn_router_b, L0_ffn_expert_w, L0_ffn_expert_b):
    import numpy as np
    import concourse.bacc as bacc
    from concourse.bass_utils import run_bass_kernel_spmd

    w = np.zeros((P, NWEIGHT), np.float32)
    wproj = np.zeros((P, P), np.float32)
    qkv_t = np.asarray(L0_conv_w_qkv).T
    small = np.zeros((P, 4), np.float32)
    eb = np.zeros((P, P), np.float32)
    for a in range(2):
        r = slice(C * a, C * a + C)
        for i, at in enumerate((WQ, WK, WV)):
            w[r, at + C * a:at + C * a + C] = qkv_t[:, C * i:C * i + C]
        w[r, WR + E * a:WR + E * a + E] = L0_ffn_router_w
        wproj[r, r] = np.asarray(L0_conv_w_proj).T
        small[r, 0] = L0_conv_b_proj
        for c in range(2):
            small[32 * c + E * a:32 * c + E * a + E, 1] = L0_ffn_router_b
        for s in range(PARTS):
            eb[16 * s + E * a:16 * s + E * a + E, r] = L0_ffn_expert_b
    w[:, WE:WE + 4 * C] = np.asarray(L0_ffn_expert_w).reshape(4, P, C).transpose(1, 0, 2).reshape(P, 4 * C)
    small[:, 2], small[:, 3] = 1e-6, 1e-5
    rows = L0_conv_bias_table.shape[0]
    table = np.zeros((2 * P, HEADS), np.float32)
    table[:rows] = L0_conv_bias_table
    table = np.ascontiguousarray(table.reshape(2, P, HEADS).transpose(1, 0, 2).reshape(P, 2 * HEADS))
    arrays = {"x": np.ascontiguousarray(x), "weights": w, "proj": wproj, "small": small, "expert_bias": eb,
              "table": table, "rel": np.ascontiguousarray(np.asarray(L0_conv_rel_index).T), "consts": constants(np),
              "select": select_matrix(np)}

    nc = bacc.Bacc("TRN2", target_bir_lowering=False, num_devices=1)
    args = [nc.dram_tensor(f"in_{n}", a.shape, mybir.dt.from_np(a.dtype), kind="ExternalInput").ap()
            for n, a in arrays.items()]
    result = nc.dram_tensor("out_0", x.shape, F32, kind="ExternalOutput").ap()
    build_program(nc, *args, result)
    r = run_bass_kernel_spmd(nc, [{f"in_{n}": a for n, a in arrays.items()}], core_ids=[0])
    return r.results[0]["out_0"]
```

```python
from contextlib import ExitStack

import concourse.bass as bass
from concourse import mybir

F32 = mybir.dt.float32
BF16 = mybir.dt.bfloat16
F32R = mybir.dt.float32r
I32 = mybir.dt.int32
ALU = mybir.AluOpType
ACT = mybir.ActivationFunctionType
AX_X = mybir.AxisListType.X

P = 128
WS = 8
N = WS * WS
HEADS, HD = 4, 16
C = HEADS * HD
E = 8
PARTS = 3
U = 4
SLOTS = 16
BIG = 3.0e38

CONSTS = {}
_at = 0
for _name, _w in (("centre", P), ("mean", P), ("ident", P), ("head", HEADS), ("pair", 32), ("tile", P),
                  ("order", E), ("row", 2), ("stat", 32)):
    CONSTS[_name] = (_at, _at + _w)
    _at += _w
NCONST = _at
WQ, WK, WV, WR, WE = 0, P, 2 * P, 3 * P, 3 * P + 32
NWEIGHT = WE + 4 * C


def build_program(nc, x, weights, proj, small, router_bias, expert_bias, table, rel, consts, select_host, out):
    B, _, H, W = x.shape
    LT = WS * W
    NW = W // WS
    STRIPS = (B // 2) * (H // WS)
    CH = LT // 2
    UNITS = NW // 2
    GROUPS = UNITS // 2
    ITEMS = 16
    x_rows = x.rearrange("b c h w -> (b c) (h w)")
    out_rows = out.rearrange("b c h w -> (b c) (h w)")
    PAIRS = B // 2

    with ExitStack() as ctx:
        def sb(name, shape, dt=F32):
            return ctx.enter_context(nc.sbuf_tensor(name, shape, dt))

        def sem(name):
            return ctx.enter_context(nc.semaphore(name))

        cst = sb("cst", [P, NCONST])
        wcen = sb("wcen", [P, NWEIGHT])
        wproj = sb("wproj", [P, P])
        rbias = sb("rbias", [P, 16])
        sml = sb("sml", [P, 4])
        ebraw = sb("ebraw", [P, P])
        ebres = sb("ebres", [P, 2, P])
        eb = sb("eb", [P, PARTS, P], BF16)
        tbraw = sb("tbraw", [P, 2, HEADS])
        tbres = sb("tbres", [P, 2, 2, HEADS])
        tb = sb("tb", [P, 2, PARTS, HEADS], BF16)
        tile_id = sb("tile_id", [P, P], F32R)
        ident_bf = sb("ident_bf", [P, P], BF16)
        select = sb("select", [P, 8, P], BF16)
        bias = sb("bias", [P, HEADS, N])
        bias_hl = sb("bias_hl", [P, HEADS, N], F32R)

        xs = [sb(f"xs{b}", [P, LT]) for b in range(4)]
        sq = [sb(f"sq{c}", [P, CH]) for c in range(2)]
        rstd = [sb(f"rstd{c}", [P, CH]) for c in range(2)]
        xr = [sb(f"xr{b}", [P, NW, N]) for b in range(2)]
        qbd = [sb(f"qbd{b}", [P, NW, 2, N]) for b in range(2)]
        kex = [sb(f"kex{b}", [P, NW, HEADS, N]) for b in range(2)]
        vbd = [sb(f"vbd{b}", [P, NW, P]) for b in range(2)]
        mx = [sb(f"mx{b}", [P, 8]) for b in range(2)]
        shifted = [sb(f"shifted{b}", [P, 8, N]) for b in range(2)]
        probs = [sb(f"probs{b}", [P, 2, HEADS * N]) for b in range(2)]
        pt = [sb(f"pt{b}", [P, 4, 2, 2, N]) for b in range(2)]
        lnd = sb("lnd", [P, 256])
        rden = [sb(f"rden{b}", [P, 256]) for b in range(2)]
        onrm = [sb(f"onrm{c}", [P, CH]) for c in range(2)]
        prj = [sb(f"prj{c}", [P, CH]) for c in range(2)]
        tt = [sb(f"tt{b}", [P, LT]) for b in range(4)]
        sq2 = [sb(f"sqb{c}", [P, CH]) for c in range(2)]
        xd = [sb(f"xd{b}", [P, 2, LT]) for b in range(2)]
        lg = sb("lg", [P, CH])
        st_ = sb("st_", [P, 4, 4, 2])
        mq = sb("mq", [P, 4, 2, 2])
        vr = sb("vr", [P, 16])
        lnr = sb("lnr", [P, 16])
        rs = sb("rs", [P, 16])
        Lr = sb("Lr", [P, 16, E])
        Ls = sb("Ls", [P, 16, E])
        L = sb("L", [P, 16, E])
        L2 = sb("L2", [P, 16, E])
        eq = sb("eq", [P, 16, E])
        cand = sb("cand", [P, 16, E])
        oh1 = sb("oh1", [P, 16, E])
        oh2 = sb("oh2", [P, 16, E])
        m1 = sb("m1", [P, 16])
        m2 = sb("m2", [P, 16])
        rk = sb("rk", [P, 16])
        dl = sb("dl", [P, 16])
        ed = sb("ed", [P, 16])
        es = sb("es", [P, 16])
        g1 = sb("g1", [P, 16])
        g2 = sb("g2", [P, 16])
        ga = sb("ga", [P, 16, E])
        gb = sb("gb", [P, 16, E])
        gr = sb("gr", [P, 2, 16, E])
        gs = sb("gs", [P, 2, 16, E])
        gp = sb("gp", [P, 8, 8, 16], BF16)
        gT = [sb(f"gT{b}", [P, LT], BF16) for b in range(2)]
        z = [sb(f"z{b}", [P, CH]) for b in range(2)]
        ob = [sb(f"ob{b}", [P, LT]) for b in range(2)]

        bank = ctx.enter_context(nc.psum_tensor("bank", [P, 8, 512], F32))
        S_BANK, PT_BANK, OD_BANK, PRE, G_BANK, Y_BANK = (0, 1), 2, 3, 4, (5, 6), 7

        def cv(name, rows=P):
            return cst[0:rows, CONSTS[name][0]:CONSTS[name][1]]

        def windows(t, c):
            v = t[:, :].rearrange("p (r w k) -> p w r k", r=WS, k=WS)
            return v[:, c * (NW // 2):(c + 1) * (NW // 2)]

        def as_windows(ap):
            return ap.rearrange("p (w r k) -> p w r k", r=WS, k=WS)

        def chunk(t, c):
            return t[:, c * (NW // 2):(c + 1) * (NW // 2), :].rearrange("p w n -> p (w n)")

        def dup(ap):
            return ap.unsqueeze(1).broadcast_to([P, 2, ap.shape[1]])

        pre_bf = bank[:, PRE, :].bitcast(BF16)
        wraw = xd[1][:, 0, 0:NWEIGHT]
        select_raw = xd[0][:, 0, :]
        rel_int = kex[0][:, :, :, :].rearrange("p w h n -> p (w h n)").bitcast(I32)
        hot = kex[1][:, :, :, :].rearrange("p w h n -> p (w h n)").bitcast(BF16)
        onehot = [hot[:, half * N * N:(half + 1) * N * N].rearrange("p (k q) -> p k q", q=N) for half in range(2)]

        loaded = sem("loaded")
        setup_dve = sem("setup_dve")
        setup_pe = sem("setup_pe")
        setup_dve_own = sem("setup_dve_own")
        rel_loaded = sem("rel_loaded")
        x_loaded = [sem(f"x_loaded{b}") for b in range(4)]
        xd_loaded = [sem(f"xd_loaded{b}") for b in range(2)]
        stored = [sem(f"stored{b}") for b in range(2)]
        centred, var_full = sem("centred"), sem("var_full")
        sq_ready, ln_done, rstd_ready, xr_ready = sem("sq_ready"), sem("ln_done"), sem("rstd_ready"), sem("xr_ready")
        q_full, k_full, v_full = sem("q_full"), sem("k_full"), sem("v_full")
        q_ready, k_ready, v_ready = sem("q_ready"), sem("k_ready"), sem("v_ready")
        s_full, max_done, shift_done, exp_done = sem("s_full"), sem("max_done"), sem("shift_done"), sem("exp_done")
        t_full, pt_ready, od_full, lnd_done, rden_ready, o_ready = (sem("t_full"), sem("pt_ready"), sem("od_full"),
                                                                  sem("lnd_done"), sem("rden_ready"), sem("o_ready"))
        prj_full, prj_ready, t_ready = sem("prj_full"), sem("prj_ready"), sem("t_ready")
        sq2_ready, stat_ready, lnr_done, rs_ready = sem("sq2_ready"), sem("stat_ready"), sem("lnr_done"), sem("rs_ready")
        lg_full, lg_ready, lgt_full, L_ready = sem("lg_full"), sem("lg_ready"), sem("lgt_full"), sem("L_ready")
        top, delta_ready, ed_ready, g_ready = sem("top"), sem("delta_ready"), sem("ed_ready"), sem("g_ready")
        gate, gp_ready, gt_full, gt_ready = sem("gate"), sem("gp_ready"), sem("gt_full"), sem("gt_ready")
        g_full, z_ready, e_done, y_ready = sem("g_full"), sem("z_ready"), sem("e_done"), sem("y_ready")

        TOP = 16
        GATE = 8

        ROUNDS = [("C0", 1, sq_ready, 2, 1), ("C1", 1, sq_ready, 2, 2), ("var0", 1, ln_done, 2, 1),
                  ("var1", 1, ln_done, 2, 2), ("proj1", -1, prj_ready, 2, 2), ("Q0", 1, q_ready, 4, 2),
                  ("K0", 1, k_ready, 2, 1), ("Q1", 1, q_ready, 4, 4), ("router", -1, lg_ready, 1, 1),
                  ("K1", 1, k_ready, 2, 2), ("V0", 1, v_ready, 8, 4), ("lgT", -1, L_ready, 2, 2),
                  ("V1", 1, v_ready, 8, 8), ("proj0", 0, prj_ready, 2, 1), ("gT", -1, gt_ready, 1, 1)]
        NAMES = [r[0] for r in ROUNDS]

        class Step:

            def __init__(self, c, n, inner):
                self.c, self.n, self.inner = c, n, inner

            def strip(self, off):
                return Strip(self.c + off, self.n, self.inner)

        class Strip:

            def __init__(self, c, n, inner):
                self.c, self.n, self.inner = c, n, inner
                self.on = inner or 0 <= c < STRIPS

            def buf(self, k):
                return self.c % k

            def count(self, per, k, lag=0):
                v = per * (self.c - lag) + k
                return v + per * U * self.n if self.inner else v

            def rounds(self, k, of):
                v = of * (self.c // k)
                return v + of * (U // k) * self.n if self.inner else v

        def wait(eng, s, value):
            if isinstance(value, int) and value <= 0:
                return
            eng.wait_ge(s, value)

        def steps(run):
            first, last = -1, STRIPS + 1
            lo = 6
            n = (STRIPS - 1 - lo) // U
            for i in range(first, lo):
                run(Step(i, 0, False))
            with nc.Fori(0, n, engines=(run.engine,)) as r:
                for v in range(U):
                    run(Step(lo + v, r, True))
            for i in range(lo + n * U, last + 1):
                run(Step(i, 0, False))

        def stepped(engine_type):
            def mark(f):
                class Run:
                    engine = engine_type

                    def __call__(self, st):
                        f(st)
                steps(Run())
            return mark

        block = ctx.enter_context(nc.Block())
        ET = mybir.EngineType

        @block.sync
        def _(sp):
            for dst, src in ((cst[:, :], consts), (wraw, weights), (wproj[:, :], proj), (sml[:, :], small), (rbias[:, :], router_bias),
                             (ebraw[:, :], expert_bias), (select_raw, select_host)):
                sp.dma_start(dst, src).then_inc(loaded, 16)
            sp.dma_start(tbraw[:, :, :].rearrange("p a h -> p (a h)"), table).then_inc(loaded, 16)
            sp.dma_start(rel_int, rel.rearrange("k q -> (k q)").partition_broadcast(P)).then_inc(rel_loaded, 16)

            def place(rows, strip):
                pr = strip.buf(PAIRS)
                return rows[pr * P:(pr + 1) * P, bass.ds(strip.rounds(PAIRS, LT), LT)]

            def load(strip):
                src = place(x_rows, strip)
                used = strip.count(2, 2, lag=4)
                wait(sp, t_ready, used)
                sp.dma_start(xs[strip.buf(4)][:, :], src).then_inc(x_loaded[strip.buf(4)], 16)

            load(Strip(0, 0, False))

            @stepped(ET.SP)
            def _(st):
                nx = st.strip(2)
                if nx.on:
                    load(nx)
                r = st.strip(-1)
                if r.on:
                    wait(sp, t_ready, r.count(2, 2))
                    for a in range(2):
                        for d in range(2):
                            sp.dma_start(xd[r.buf(2)][64 * d:64 * d + 64, a, :],
                                         tt[r.buf(4)][64 * a:64 * a + 64, :]).then_inc(xd_loaded[r.buf(2)], 16)
                m = st.strip(-2)
                if m.on:
                    dst, summed = place(out_rows, m), m.count(2, 2)
                    wait(sp, y_ready, summed)
                    sp.dma_start(dst, ob[m.buf(2)][:, :]).then_inc(stored[m.buf(2)], 16)

            for b in range(2):
                sp.wait_ge(stored[b], 16 * (STRIPS // 2))

        @block.tensor
        def _(pe):
            mm = nc.tensor.matmul
            pe.wait_ge(loaded, 128)
            mm(bank[:, 0, 0:WR], cv("centre"), wraw[:, 0:WR], start=True, stop=True)
            mm(bank[:, 1, 0:NWEIGHT - WR], cv("centre"), wraw[:, WR:NWEIGHT], start=True, stop=True).then_inc(setup_pe, 1)
            pe.wait_ge(setup_dve, 5)
            for k in range(N):
                for q in (0, N):
                    dst = bank[q:q + N, 2 + k // 32, 12 * (k % 32):12 * (k % 32) + 12]
                    for half in range(2):
                        last = mm(dst, onehot[half][:, k, :], tb[:, half, :, :].rearrange("p s h -> p (s h)"),
                                  start=(half == 0), stop=(half == 1), skip_group_check=True)
            last.then_inc(setup_pe, 1)
            pe.wait_ge(setup_dve, 7)

            def pre_free(st, name):
                at, c = NAMES.index(name), st.c
                while True:
                    at -= 1
                    if at < 0:
                        at, c = len(ROUNDS) - 1, c - 1
                    if c < -1:
                        return
                    _, off, s, per, k = ROUNDS[at]
                    if st.inner or 0 <= c + off < STRIPS:
                        wait(pe, s, Strip(c + off, st.n, st.inner).count(per, k))
                        return

            def scores(st, u):
                s = st.strip(0)
                b = bank[:, S_BANK[u % 2], :]
                if u % 4 == 0:
                    pe.wait_ge(q_ready, s.count(4, 2 * (u // 4) + 2))
                    pe.wait_ge(k_ready, s.count(2, u // 4 + 1))
                wait(pe, shift_done, s.count(UNITS, u - 1))
                mm(b, tile_id[:, :], dup(bias_hl[:, :, :].rearrange("p h k -> p (h k)")), start=True, stop=False,
                   skip_group_check=True)
                for j in range(2):
                    w = 2 * u + j
                    last = mm(b[:, 256 * j:256 * j + 256], qbd[s.buf(2)][:, w, :, :].rearrange("p a q -> p (a q)"),
                              kex[s.buf(2)][:, w, :, :].rearrange("p h k -> p (h k)"), start=False, stop=(j == 1),
                              skip_group_check=True)
                last.then_inc(s_full, 1)

            def transposes(s, u):
                pe.wait_ge(exp_done, s.count(UNITS, u + 1))
                wait(pe, pt_ready, s.count(UNITS, u))
                for j in range(4):
                    last = nc.tensor.transpose(bank[:, PT_BANK, 128 * j:128 * j + 128],
                                               probs[u % 2][:, j // 2, 128 * (j % 2):128 * (j % 2) + 128], cv("ident"))
                last.then_inc(t_full, 1)

            def values(s, u):
                g = u // 2
                pe.wait_ge(pt_ready, s.count(UNITS, u + 1))
                if u % 2 == 0:
                    pe.wait_ge(v_ready, s.count(8, 4 * (g // 2) + 4))
                    wait(pe, o_ready, s.count(GROUPS, g))
                for wl in range(2):
                    w4 = 2 * (u % 2) + wl
                    for a in range(2):
                        for j in range(2):
                            q = 64 * a + 32 * j
                            last = mm(bank[q:q + 32, OD_BANK, N * w4:N * w4 + N], vbd[s.buf(2)][:, 2 * u + wl, q:q + 32],
                                      pt[g % 2][:, w4, j, a, :], start=True, stop=True, skip_group_check=True)
                if u % 2 == 1:
                    for a in range(2):
                        for j in range(2):
                            q = 64 * a + 32 * j
                            last = mm(bank[q:q + 32, OD_BANK, 256:512], cv("pair"), pt[g % 2][:, :, j, a, :],
                                      start=True, stop=True, skip_group_check=True)
                    last.then_inc(od_full, 1)

            def project(st, s, c, name):
                pe.wait_ge(o_ready, s.count(GROUPS, 2 * c + 2))
                pre_free(st, name)
                mm(bank[:, PRE, :], wproj[:, :], onrm[c][:, :], start=True, stop=True).then_inc(prj_full, 1)

            def gates_wide(s, n):
                c, j, a = n // 8, n % 8 // 2, n % 2
                if n == 0:
                    pe.wait_ge(gt_ready, s.count(1, 1))
                wait(pe, z_ready, s.count(ITEMS, n - 1))
                mm(bank[:, G_BANK[n % 2], :], select[:, 4 * a + j, :], gT[s.buf(2)][:, c * CH:(c + 1) * CH],
                   start=True, stop=True).then_inc(g_full, 1)

            def experts(s, n):
                c, j, a = n // 8, n % 8 // 2, n % 2
                if n % 8 == 0:
                    wait(pe, y_ready, s.count(2, c))
                    for k in range(PARTS):
                        mm(bank[:, Y_BANK, :], eb[:, k, :], gT[s.buf(2)][:, c * CH:(c + 1) * CH],
                           start=(k == 0), stop=False, skip_group_check=True)
                pe.wait_ge(z_ready, s.count(ITEMS, n + 1))
                mm(bank[64 * a:64 * a + 64, Y_BANK, :], wcen[:, WE + C * j:WE + C * j + C], z[n % 2][:, :],
                   start=False, stop=(j == 3), skip_group_check=True).then_inc(e_done, 1)

            @stepped(ET.PE)
            def _(st):
                pre, att, old, moe = st.strip(1), st.strip(0), st.strip(-1), st.strip(-2)
                for k in range(SLOTS):
                    if k % 2 == 0 and att.on:
                        scores(st, k // 2)
                    if k in (0, 1) and pre.on:
                        if k == 0:
                            pe.wait_ge(x_loaded[pre.buf(4)], pre.rounds(4, 16) + 16)
                        pre_free(st, f"C{k}")
                        mm(bank[:, PRE, :], cv("centre"), windows(xs[pre.buf(4)], k), start=True,
                           stop=True).then_inc(centred, 1)
                    if k in (2, 3) and pre.on:
                        pe.wait_ge(sq_ready, pre.count(2, k - 1))
                        pre_free(st, f"var{k - 2}")
                        mm(bank[:, PRE, :], cv("mean"), sq[k - 2][:, :], start=True, stop=True).then_inc(var_full, 1)
                    if k == 4 and old.on:
                        project(st, old, 1, "proj1")
                    if k in (5, 7) and pre.on:
                        c = (k - 5) // 2
                        pe.wait_ge(xr_ready, pre.count(2, c + 1))
                        pre_free(st, f"Q{c}")
                        mm(bank[:, PRE, :], wcen[:, WQ:WQ + P], chunk(xr[pre.buf(2)], c), start=True,
                           stop=True).then_inc(q_full, 1)
                    if k == 8 and old.on:
                        pe.wait_ge(t_ready, old.count(2, 2))
                        pe.wait_ge(sq2_ready, old.count(2, 2))
                        pre_free(st, "router")
                        for c in range(2):
                            mm(bank[32 * c:32 * c + 32, PRE, :], wcen[:, WR:WR + 32],
                               tt[old.buf(4)][:, c * CH:(c + 1) * CH], start=True, stop=True)
                        for c in range(2):
                            last = mm(bank[64 + 32 * c:96 + 32 * c, PRE, :], cv("stat"), sq2[c][:, :], start=True,
                                      stop=True)
                        last.then_inc(lg_full, 1)
                    if k in (6, 8) and pre.on:
                        c = (k - 6) // 2
                        pre_free(st, f"K{c}")
                        mm(bank[:, PRE, :], wcen[:, WK:WK + P], chunk(xr[pre.buf(2)], c), start=True,
                           stop=True).then_inc(k_full, 1)
                    if k in (9, 11) and pre.on:
                        c = (k - 9) // 2
                        pre_free(st, f"V{c}")
                        for pair in range(4):
                            w = 8 * c + 2 * pair
                            last = mm(bank[:, PRE, 128 * pair:128 * pair + 128],
                                      xr[pre.buf(2)][:, w:w + 2, :].rearrange("p w n -> p (w n)"),
                                      wcen[:, WV:WV + P], start=True, stop=True)
                        last.then_inc(v_full, 1)
                    if k == 10 and old.on:
                        pe.wait_ge(lg_ready, old.count(1, 1))
                        pre_free(st, "lgT")
                        for ttl in range(4):
                            last = nc.tensor.transpose(bank[:, PRE, 128 * ttl:128 * ttl + 128],
                                                       lg[:, 128 * ttl:128 * ttl + 128], cv("ident"))
                        last.then_inc(lgt_full, 1)
                    if k == 12 and att.on:
                        project(st, att, 0, "proj0")
                    if k == 15 and old.on:
                        pe.wait_ge(gp_ready, old.count(1, 1))
                        pre_free(st, "gT")
                        for t8 in range(8):
                            ttl, c = t8 // 2, t8 % 2
                            last = nc.tensor.transpose(pre_bf[:, c * CH + 128 * ttl:c * CH + 128 * ttl + 128],
                                                       gp[:, t8, :, :].rearrange("p s e -> p (s e)"), ident_bf[:, :])
                        last.then_inc(gt_full, 1)
                    if k == 0 and old.on:
                        transposes(old, 7)
                    if k == 1 and old.on:
                        values(old, 7)
                    if att.on:
                        if k % 2 == 0 and k >= 2:
                            transposes(att, k // 2 - 1)
                        if k % 2 == 1 and k >= 3:
                            values(att, (k - 3) // 2)
                    if moe.on:
                        gates_wide(moe, k)
                        if k:
                            experts(moe, k - 1)
                        if k == SLOTS - 1:
                            experts(moe, k)

        @block.scalar
        def _(act):
            af = nc.scalar.activation
            nc.scalar.preload_act_table_set("natural_log_exp_and_others")
            act.wait_ge(loaded, 128)

            def exps(s, u):
                act.wait_ge(shift_done, s.count(UNITS, u + 1))
                wait(act, t_full, s.count(UNITS, u - 1))
                af(probs[u % 2][:, :, :].rearrange("p w k -> p (w k)"),
                   shifted[u % 2][:, :, :].rearrange("p g k -> p (g k)"), ACT.Exp).then_inc(exp_done, 1)

            def move_pt(s, u):
                g = u // 2
                act.wait_ge(t_full, s.count(UNITS, u + 1))
                if u % 2 == 0:
                    wait(act, od_full, s.count(GROUPS, g - 1))
                af(pt[g % 2][:, 2 * (u % 2):2 * (u % 2) + 2, :, :, :].rearrange("p w j a q -> p (w j a q)"),
                   bank[:, PT_BANK, :], ACT.Copy).then_inc(pt_ready, 1)

            def inverse_sums(s, g):
                act.wait_ge(od_full, s.count(GROUPS, g + 1))
                wait(act, rden_ready, s.count(GROUPS, g))
                af(lnd[:, :], bank[:, OD_BANK, 256:512], ACT.Ln).then_inc(lnd_done, 1)
                act.wait_ge(lnd_done, s.count(GROUPS, g + 1))
                wait(act, o_ready, s.count(GROUPS, g - 1))
                af(rden[g % 2][:, :], lnd[:, :], ACT.Exp, scale=-1.0).then_inc(rden_ready, 1)

            def square(s, c):
                act.wait_ge(centred, s.count(2, c + 1))
                wait(act, rstd_ready, s.count(2, c + 1, lag=1))
                af(sq[c][:, :], bank[:, PRE, :], ACT.Square).then_inc(sq_ready, 1)

            def inverse_std(s, c):
                act.wait_ge(var_full, s.count(2, c + 1))
                af(sq[c][:, :], bank[:, PRE, :], ACT.Ln, bias=sml[:, 2:3]).then_inc(ln_done, 1)
                act.wait_ge(ln_done, s.count(2, c + 1))
                wait(act, xr_ready, s.count(2, c + 1, lag=1))
                af(rstd[c][:, :], sq[c][:, :], ACT.Exp, scale=-0.5).then_inc(rstd_ready, 1)

            def square_residual(s, c):
                act.wait_ge(t_ready, s.count(2, c + 1))
                wait(act, lg_full, s.count(1, 1, lag=1))
                af(sq2[c][:, :], tt[s.buf(4)][:, c * CH:(c + 1) * CH], ACT.Square).then_inc(sq2_ready, 1)

            def move_proj(s, c):
                act.wait_ge(prj_full, s.count(2, c + 1))
                wait(act, t_ready, s.count(2, c + 1, lag=1))
                af(prj[c][:, :], bank[:, PRE, :], ACT.Identity, bias=sml[:, 0:1]).then_inc(prj_ready, 1)

            @stepped(ET.Activation)
            def _(st):
                pre, att, old = st.strip(1), st.strip(0), st.strip(-1)
                for k in range(SLOTS):
                    if k % 2 == 1 and att.on:
                        exps(att, k // 2)
                    if k in (0, 1) and pre.on:
                        square(pre, k)
                    if k == 0 and old.on:
                        move_pt(old, 7)
                        square_residual(old, 0)
                    if k == 1 and old.on:
                        inverse_sums(old, 3)
                    if k in (2, 3) and pre.on:
                        inverse_std(pre, k - 2)
                    if k == 4 and old.on:
                        move_proj(old, 1)
                    if k in (5, 7) and pre.on:
                        c = (k - 5) // 2
                        act.wait_ge(q_full, pre.count(2, c + 1))
                        wait(act, s_full, pre.count(UNITS, UNITS, lag=2))
                        for a in range(2):
                            af(qbd[pre.buf(2)][64 * a:64 * a + 64, 8 * c:8 * c + 8, a, :],
                               bank[64 * a:64 * a + 64, PRE, :].rearrange("p (w q) -> p w q", q=N), ACT.Copy,
                               scale=float(HD) ** -0.5).then_inc(q_ready, 1)
                    if k == 6 and old.on:
                        square_residual(old, 1)
                    if k == 8 and old.on:
                        act.wait_ge(lg_full, old.count(1, 1))
                        wait(act, lgt_full, old.count(1, 1, lag=1))
                        af(lg[:, :], bank[:, PRE, :], ACT.Copy).then_inc(lg_ready, 1)
                    if k in (9, 11) and pre.on:
                        c = (k - 9) // 2
                        act.wait_ge(v_full, pre.count(2, c + 1))
                        wait(act, od_full, pre.count(GROUPS, GROUPS, lag=2))
                        for wp in range(2):
                            src = bank[64 * wp:64 * wp + 64, PRE, :].rearrange("p (w m h d) -> p w m h d", w=4, h=2, d=HD)
                            for h in range(2):
                                dst = vbd[pre.buf(2)][64 * h:64 * h + 64, 8 * c + wp:8 * c + 8:2, :].rearrange(
                                    "p w (m h d) -> p w m h d", h=2, d=HD)
                                af(dst[:, :, :, h, :], src[:, :, :, h, :], ACT.Copy).then_inc(v_ready, 1)
                    if k == 11 and old.on:
                        act.wait_ge(stat_ready, old.count(1, 1))
                        af(lnr[:, :], vr[:, :], ACT.Ln).then_inc(lnr_done, 1)
                        act.wait_ge(lnr_done, old.count(1, 1))
                        wait(act, gp_ready, old.count(1, 1, lag=1))
                        af(rs[:, :], lnr[:, :], ACT.Exp, scale=-0.5).then_inc(rs_ready, 1)
                    if k == 12 and att.on:
                        move_proj(att, 0)
                    if k == 12 and old.on:
                        act.wait_ge(delta_ready, old.count(1, 1))
                        af(ed[:, :], dl[:, :], ACT.Exp).then_inc(ed_ready, 1)
                    if att.on:
                        if k % 2 == 0 and k >= 2:
                            move_pt(att, k // 2 - 1)
                        if k % 4 == 1 and k >= 5:
                            inverse_sums(att, (k - 5) // 4)

        @block.gpsimd
        def _(pool):
            tt_ = nc.gpsimd.tensor_tensor
            for b in range(2):
                nc.gpsimd.memset(qbd[b][:, :, :, :], 0.0).then_inc(setup_dve, 1)

            @stepped(ET.Pool)
            def _(st):
                pre, att, old, moe = st.strip(1), st.strip(0), st.strip(-1), st.strip(-2)

                def residual(s, c):
                    pool.wait_ge(prj_ready, s.count(2, c + 1))
                    wait(pool, y_ready, s.count(2, c + 1, lag=4))
                    if c == 1:
                        wait(pool, z_ready, s.count(ITEMS, ITEMS, lag=2))
                    tt_(as_windows(tt[s.buf(4)][:, c * CH:(c + 1) * CH]), as_windows(prj[c][:, :]),
                        windows(xs[s.buf(4)], c), op=ALU.add).then_inc(t_ready, 1)

                def scale_x(c):
                    pool.wait_ge(rstd_ready, pre.count(2, c + 1))
                    if c == 0:
                        pool.wait_ge(x_loaded[pre.buf(4)], pre.rounds(4, 16) + 16)
                    wait(pool, v_ready, pre.count(8, 8, lag=2))
                    tt_(as_windows(chunk(xr[pre.buf(2)], c)), windows(xs[pre.buf(4)], c),
                        as_windows(rstd[c][:, :]), op=ALU.mult).then_inc(xr_ready, 1)

                if pre.on:
                    scale_x(0)
                    scale_x(1)
                if old.on:
                    residual(old, 1)
                if old.on:
                    wide = lambda ap: ap.unsqueeze(2).broadcast_to([P, 16, E])
                    part = lambda n: gp[:, :, 2 * n:2 * n + 2, :].rearrange("p t q m -> p q t m")
                    v4 = lambda t: t[:, :, :, :].rearrange("p q (t a) e -> p q t (a e)", a=2)
                    v3 = lambda ap: ap.rearrange("p (t a) e -> p t (a e)", a=2)
                    pool.wait_ge(g_ready, old.count(2, 2))
                    wait(pool, gt_full, old.count(1, 1, lag=1))
                    tt_(ga[:, :, :], oh1[:, :, :], wide(g1[:, :]), op=ALU.mult).then_inc(gate, 1)
                    tt_(gb[:, :, :], oh2[:, :, :], wide(g2[:, :]), op=ALU.mult).then_inc(gate, 1)
                    pool.wait_ge(gate, old.count(GATE, 2))
                    tt_(gr[:, 0, :, :], ga[:, :, :], gb[:, :, :], op=ALU.add).then_inc(gate, 1)
                    tt_(gp[:, :, 0, :], v3(ga[:, :, :]), v3(gb[:, :, :]), op=ALU.add).then_inc(gate, 1)
                    pool.wait_ge(rs_ready, old.count(1, 1))
                    pool.wait_ge(gate, old.count(GATE, 3))
                    tt_(gr[:, 1, :, :], gr[:, 0, :, :], wide(rs[:, :]), op=ALU.mult).then_inc(gate, 1)
                    tt_(gp[:, :, 1, :].rearrange("p t (a e) -> p t a e", a=2),
                        gr[:, 0, :, :].rearrange("p (t a) e -> p t a e", a=2),
                        rs[:, :].rearrange("p (t a) -> p t a", a=2).unsqueeze(3).broadcast_to([P, 8, 2, E]),
                        op=ALU.mult).then_inc(gate, 1)
                    pool.wait_ge(gate, old.count(GATE, 6))
                    tt_(v4(gs), v4(gr), part(0), op=ALU.subtract).then_inc(gate, 1)
                    tt_(part(1), v4(gr), part(0), op=ALU.subtract).then_inc(gate, 1)
                    pool.wait_ge(gate, old.count(GATE, 8))
                    tt_(part(2), v4(gs), part(1), op=ALU.subtract).then_inc(gp_ready, 1)
                if att.on:
                    residual(att, 0)

        @block.vector
        def _(dve):
            tt_, red = nc.vector.tensor_tensor, nc.vector.tensor_reduce
            copy = nc.vector.tensor_copy
            dve.wait_ge(loaded, 128)
            dve.wait_ge(setup_pe, 1)
            dve.wait_ge(setup_dve, 2)
            copy(wcen[:, 0:WR], bank[:, 0, 0:WR])
            tt_(wcen[:, WR:WR + 32], bank[:, 1, 0:32], cv("stat"), op=ALU.add)
            copy(wcen[:, WE:NWEIGHT], bank[:, 1, 32:NWEIGHT - WR])
            copy(tile_id[:, :], cv("tile"))
            copy(ident_bf[:, :], cv("ident"))
            copy(select[:, :, :].rearrange("p s n -> p (s n)"), select_raw)
            for b in range(2):
                nc.vector.memset(vbd[b][:, :, :], 0.0)
            nc.vector.memset(gp[:, :, :, :], 0.0)
            nc.vector.memset(lg[:, :], 0.0)

            def link(ins, n):
                ins.then_inc(setup_dve_own, 1)
                dve.wait_ge(setup_dve_own, n)

            link(copy(eb[:, 0, :], ebraw[:, :]), 1)
            link(tt_(ebres[:, 0, :], ebraw[:, :], eb[:, 0, :], op=ALU.subtract), 2)
            link(copy(eb[:, 1, :], ebres[:, 0, :]), 3)
            link(tt_(eb[:, 2, :], ebres[:, 0, :], eb[:, 1, :], op=ALU.subtract), 4)
            link(copy(tb[:, :, 0, :], tbraw[:, :, :]), 5)
            link(tt_(tbres[:, 0, :, :], tbraw[:, :, :], tb[:, :, 0, :], op=ALU.subtract), 6)
            link(copy(tb[:, :, 1, :], tbres[:, 0, :, :]), 7)
            tt_(tb[:, :, 2, :], tbres[:, 0, :, :], tb[:, :, 1, :], op=ALU.subtract).then_inc(setup_dve, 1)
            dve.wait_ge(rel_loaded, 16)
            for half in range(2):
                nc.vector.tensor_scalar(onehot[half].rearrange("p k q -> p (k q)"), rel_int,
                                        cv("row")[:, half:half + 1], None, ALU.is_equal).then_inc(setup_dve, 1)
            dve.wait_ge(setup_pe, 2)
            for kh in range(2):
                src = bank[:, 2 + kh, 0:384].rearrange("p (k s h) -> p s h k", s=PARTS, h=HEADS)
                link(copy(bias[:, :, 32 * kh:32 * kh + 32], src[:, 2, :, :]), 8 + 3 * kh)
                for n, part in enumerate((1, 0)):
                    link(tt_(bias[:, :, 32 * kh:32 * kh + 32], bias[:, :, 32 * kh:32 * kh + 32], src[:, part, :, :],
                             op=ALU.add), 9 + 3 * kh + n)
            copy(bias_hl[:, :, :], bias[:, :, :]).then_inc(setup_dve, 1)
            dve.wait_ge(setup_dve, 6)
            tt_(bias_hl[64:128, :, :], bias[64:128, :, :], bias_hl[64:128, :, :].bitcast(F32),
                op=ALU.subtract).then_inc(setup_dve, 1)

            def softmax_shift(s, u):
                b = bank[:, S_BANK[u % 2], :].rearrange("p (g k) -> p g k", k=N)
                dve.wait_ge(s_full, s.count(UNITS, u + 1))
                red(mx[u % 2][:, :], b, axis=AX_X, op=ALU.max).then_inc(max_done, 1)
                dve.wait_ge(max_done, s.count(UNITS, u + 1))
                wait(dve, exp_done, s.count(UNITS, u - 1))
                tt_(shifted[u % 2][:, :, :], b, mx[u % 2][:, :].unsqueeze(2).broadcast_to([P, 8, N]),
                    op=ALU.subtract).then_inc(shift_done, 1)

            def normalise(s, g):
                dve.wait_ge(rden_ready, s.count(GROUPS, g + 1))
                c = g // 2
                wait(dve, prj_full, s.count(2, c + 1, lag=1))
                tt_(onrm[c][:, 256 * (g % 2):256 * (g % 2) + 256], bank[:, OD_BANK, 0:256], rden[g % 2][:, :],
                    op=ALU.mult).then_inc(o_ready, 1)

            def gated(s, n):
                c, a = n // 8, n % 2
                dve.wait_ge(g_full, s.count(ITEMS, n + 1))
                if n == 0:
                    dve.wait_ge(xd_loaded[s.buf(2)], s.rounds(2, 64) + 64)
                wait(dve, e_done, s.count(ITEMS, n - 1))
                tt_(z[n % 2][:, :], bank[:, G_BANK[n % 2], :], xd[s.buf(2)][:, a, c * CH:(c + 1) * CH],
                    op=ALU.mult).then_inc(z_ready, 1)

            def finish(s, c):
                dve.wait_ge(e_done, s.count(ITEMS, 8 * c + 8))
                if c == 0:
                    wait(dve, stored[s.buf(2)], s.rounds(2, 16))
                tt_(windows(ob[s.buf(2)], c), as_windows(bank[:, Y_BANK, :]),
                    as_windows(tt[s.buf(4)][:, c * CH:(c + 1) * CH]), op=ALU.add).then_inc(y_ready, 1)

            def top_two(s):
                n = [0]

                def step(ins):
                    n[0] += 1
                    ins.then_inc(top, 1)
                    dve.wait_ge(top, s.count(TOP, n[0]))

                wide = lambda ap: ap.unsqueeze(2).broadcast_to([P, 16, E])
                order = cv("order").unsqueeze(1).broadcast_to([P, 16, E])

                def pick(vals, m, oh):
                    step(red(m[:, :], vals[:, :, :], axis=AX_X, op=ALU.max))
                    step(tt_(eq[:, :, :], vals[:, :, :], wide(m[:, :]), op=ALU.is_equal))
                    step(tt_(cand[:, :, :], eq[:, :, :], order, op=ALU.mult))
                    step(red(rk[:, :], cand[:, :, :], axis=AX_X, op=ALU.max))
                    step(tt_(oh[:, :, :], cand[:, :, :], wide(rk[:, :]), op=ALU.is_equal))

                step(tt_(mq[:, :, :, :], st_[:, :, 0:2, :], st_[:, :, 0:2, :], op=ALU.mult))
                step(tt_(vr[:, :].rearrange("p (t m) -> p t m", m=4), st_[:, :, 2:4, :].rearrange("p t c a -> p t (c a)"),
                         mq[:, :, :, :].rearrange("p t c a -> p t (c a)"), op=ALU.subtract))
                nc.vector.tensor_scalar(vr[:, :], vr[:, :], 0.0, 1e-5, ALU.max, ALU.add).then_inc(stat_ready, 1)
                dve.wait_ge(rs_ready, s.count(1, 1))
                step(tt_(Ls[:, :, :], Lr[:, :, :], wide(rs[:, :]), op=ALU.mult))
                step(tt_(L[:, :, :].rearrange("p (t a) e -> p t (a e)", a=2),
                         Ls[:, :, :].rearrange("p (t a) e -> p t (a e)", a=2),
                         rbias[:, :].unsqueeze(1).broadcast_to([P, 8, 16]), op=ALU.add))
                wait(dve, gp_ready, s.count(1, 1, lag=1))
                pick(L, m1, oh1)
                step(nc.vector.scalar_tensor_tensor(out=L2[:, :, :], in0=oh1[:, :, :], scalar=-BIG, in1=L[:, :, :],
                                                    op0=ALU.mult, op1=ALU.add))
                pick(L2, m2, oh2)
                tt_(dl[:, :], m2[:, :], m1[:, :], op=ALU.subtract).then_inc(delta_ready, 1)
                dve.wait_ge(ed_ready, s.count(1, 1))
                step(nc.vector.tensor_scalar(es[:, :], ed[:, :], 1.0, None, ALU.add))
                nc.vector.reciprocal(g1[:, :], es[:, :]).then_inc(g_ready, 1)
                dve.wait_ge(g_ready, s.count(2, 1))
                tt_(g2[:, :], ed[:, :], g1[:, :], op=ALU.mult).then_inc(g_ready, 1)
                assert n[0] == TOP

            @stepped(ET.DVE)
            def _(st):
                pre, att, old, moe = st.strip(1), st.strip(0), st.strip(-1), st.strip(-2)
                for k in range(SLOTS):
                    if k % 2 == 0 and att.on:
                        softmax_shift(att, k // 2)
                    if k == 1 and old.on:
                        normalise(old, 3)
                    if k in (6, 8) and pre.on:
                        c = (k - 6) // 2
                        dve.wait_ge(k_full, pre.count(2, c + 1))
                        wait(dve, s_full, pre.count(UNITS, UNITS, lag=2))
                        src = bank[:, PRE, :].rearrange("p (w n) -> p w n", n=N)
                        for h in range(0, HEADS):
                            last = nc.vector.tensor_scalar(kex[pre.buf(2)][:, 8 * c:8 * c + 8, h, :], src,
                                                           cv("head")[:, h:h + 1], None, ALU.mult)
                        last.then_inc(k_ready, 1)
                    if k == 10 and old.on:
                        dve.wait_ge(lgt_full, old.count(1, 1))
                        src = bank[:, PRE, :].rearrange("p (t c m) -> p t c m", t=4, m=32)
                        copy(Lr[:, :, :].rearrange("p (t c a) e -> p t c (a e)", a=2, c=2),
                             src[:, :, 0:2, 0:16]).then_inc(L_ready, 1)
                        copy(st_[:, :, :, :], src[:, :, :, 16:18]).then_inc(L_ready, 1)
                        dve.wait_ge(L_ready, old.count(2, 2))
                    if k % 4 == 1 and k >= 5 and att.on:
                        normalise(att, (k - 5) // 4)
                    if k == 15 and old.on:
                        dve.wait_ge(gt_full, old.count(1, 1))
                        copy(gT[old.buf(2)][:, :], pre_bf[:, :]).then_inc(gt_ready, 1)
                    if moe.on:
                        gated(moe, k)
                        if k == 8:
                            finish(moe, 0)
                        if k == 15:
                            finish(moe, 1)
                    if k == 11 and old.on:
                        top_two(old)


def constants(np):
    p = np.arange(P)
    a, ch = p // C, p % C
    same = a[:, None] == a[None, :]
    parts = {
        "centre": np.eye(P) - same / C,
        "mean": same / C,
        "ident": np.eye(P),
        "head": ch[:, None] // HD == np.arange(HEADS)[None, :],
        "pair": p[:, None] // N == np.arange(32)[None, :] // HD,
        "tile": p[:, None] % N == p[None, :] % N,
        "order": np.broadcast_to(np.arange(E, 0, -1), (P, E)),
        "row": p[:, None] + P * np.arange(2)[None, :],
        "stat": (np.arange(32)[None, :] == 16 + a[:, None]) / C,
    }
    c = np.zeros((P, NCONST), np.float32)
    for name, (lo, hi) in CONSTS.items():
        c[:, lo:hi] = parts[name]
    return c


def select_matrix(np):
    p = np.arange(P)
    cols = np.arange(8 * P)
    img, pair, e2 = cols // (4 * P), cols // P % 4, cols % P // C
    return ((p[:, None] % 32 == (16 + 8 * img + 2 * pair + e2)[None, :]) & (p[:, None] < 32 * PARTS)).astype(np.float32)


def kernel(x, L0_conv_w_qkv, L0_conv_bias_table, L0_conv_w_proj, L0_conv_b_proj, L0_conv_rel_index,
           L0_ffn_router_w, L0_ffn_router_b, L0_ffn_expert_w, L0_ffn_expert_b):
    import numpy as np
    import concourse.bacc as bacc
    from concourse.bass_utils import run_bass_kernel_spmd

    w = np.zeros((P, NWEIGHT), np.float32)
    wproj = np.zeros((P, P), np.float32)
    qkv_t = np.asarray(L0_conv_w_qkv).T
    small = np.zeros((P, 4), np.float32)
    eb = np.zeros((P, P), np.float32)
    for a in range(2):
        r = slice(C * a, C * a + C)
        for i, at in enumerate((WQ, WK, WV)):
            w[r, at + C * a:at + C * a + C] = qkv_t[:, C * i:C * i + C]
        w[r, WR + E * a:WR + E * a + E] = L0_ffn_router_w
        wproj[r, r] = np.asarray(L0_conv_w_proj).T
        small[r, 0] = L0_conv_b_proj
        for s in range(PARTS):
            eb[32 * s + E * a:32 * s + E * a + E, r] = L0_ffn_expert_b
    w[:, WE:WE + 4 * C] = np.asarray(L0_ffn_expert_w).reshape(4, P, C).transpose(1, 0, 2).reshape(P, 4 * C)
    small[:, 2] = 1e-6
    router_bias = np.zeros((P, 2 * E), np.float32)
    router_bias[:] = np.tile(np.asarray(L0_ffn_router_b), 2)
    rows = L0_conv_bias_table.shape[0]
    table = np.zeros((2 * P, HEADS), np.float32)
    table[:rows] = L0_conv_bias_table
    table = np.ascontiguousarray(table.reshape(2, P, HEADS).transpose(1, 0, 2).reshape(P, 2 * HEADS))
    arrays = {"x": np.ascontiguousarray(x), "weights": w, "proj": wproj, "small": small, "router_bias": router_bias, "expert_bias": eb,
              "table": table, "rel": np.ascontiguousarray(np.asarray(L0_conv_rel_index).T), "consts": constants(np),
              "select": select_matrix(np)}

    nc = bacc.Bacc("TRN2", target_bir_lowering=False, num_devices=1)
    args = [nc.dram_tensor(f"in_{n}", a.shape, mybir.dt.from_np(a.dtype), kind="ExternalInput").ap()
            for n, a in arrays.items()]
    result = nc.dram_tensor("out_0", x.shape, F32, kind="ExternalOutput").ap()
    build_program(nc, *args, result)
    r = run_bass_kernel_spmd(nc, [{f"in_{n}": a for n, a in arrays.items()}], core_ids=[0])
    return r.results[0]["out_0"]
```

```python
from contextlib import ExitStack

import concourse.bass as bass
from concourse import mybir

F32 = mybir.dt.float32
BF16 = mybir.dt.bfloat16
F32R = mybir.dt.float32r
I32 = mybir.dt.int32
ALU = mybir.AluOpType
ACT = mybir.ActivationFunctionType
AX_X = mybir.AxisListType.X

P = 128
WS = 8
N = WS * WS
HEADS, HD = 4, 16
C = HEADS * HD
E = 8
PARTS = 3
U = 4
SLOTS = 16
BIG = 3.0e38

CONSTS = {}
_at = 0
for _name, _w in (("centre", P), ("spread", 2 * P), ("ident", P), ("head", HEADS), ("pair", 32), ("tile", P),
                  ("order", E), ("row", 2), ("stat", 32)):
    CONSTS[_name] = (_at, _at + _w)
    _at += _w
NCONST = _at
WQ, WK, WV, WR, WE = 0, P, 2 * P, 3 * P, 3 * P + 32
NWEIGHT = WE + 4 * C


def build_program(nc, x, weights, proj, small, router_bias, expert_bias, table, rel, consts, select_host, out):
    B, _, H, W = x.shape
    LT = WS * W
    NW = W // WS
    STRIPS = (B // 2) * (H // WS)
    CH = LT // 2
    UNITS = NW // 2
    GROUPS = UNITS // 2
    ITEMS = 16
    x_rows = x.rearrange("b c h w -> (b c) (h w)")
    out_rows = out.rearrange("b c h w -> (b c) (h w)")
    PAIRS = B // 2

    with ExitStack() as ctx:
        def sb(name, shape, dt=F32):
            return ctx.enter_context(nc.sbuf_tensor(name, shape, dt))

        def sem(name):
            return ctx.enter_context(nc.semaphore(name))

        cst = sb("cst", [P, NCONST])
        wcen = sb("wcen", [P, NWEIGHT])
        wproj = sb("wproj", [P, P])
        rbias = sb("rbias", [P, 16])
        sml = sb("sml", [P, 4])
        ebraw = sb("ebraw", [P, P])
        ebres = sb("ebres", [P, P])
        ebmid = sb("ebmid", [P, P], BF16)
        eb = sb("eb", [P, 2, P], BF16)
        tbraw = sb("tbraw", [P, 2, HEADS])
        tbres = sb("tbres", [P, 2, HEADS])
        tb = sb("tb", [P, 2, PARTS, HEADS], BF16)
        tile_id = sb("tile_id", [P, P], F32R)
        ident_bf = sb("ident_bf", [P, P], BF16)
        select = sb("select", [P, 8, P], BF16)
        bias = sb("bias", [P, HEADS, N])
        bias_hl = sb("bias_hl", [P, HEADS, N], F32R)

        xs = [sb(f"xs{b}", [P, LT]) for b in range(4)]
        sq = [sb(f"sq{c}", [P, CH]) for c in range(2)]
        msq = sb("msq", [P, CH])
        var = sb("var", [P, CH])
        var_hl = sb("var_hl", [P, CH], F32R)
        spread = sb("spread", [P, 2, P], F32R)
        xr = [sb(f"xr{b}", [P, NW, N]) for b in range(2)]
        qbd = [sb(f"qbd{b}", [P, NW, 2, N]) for b in range(2)]
        kex = [sb(f"kex{b}", [P, NW, HEADS, N]) for b in range(2)]
        vbd = [sb(f"vbd{b}", [P, NW, P]) for b in range(2)]
        kr = sb("kr", [P, CH])
        mx = [sb(f"mx{b}", [P, 8]) for b in range(2)]
        shifted = [sb(f"shifted{b}", [P, 8, N]) for b in range(2)]
        probs = [sb(f"probs{b}", [P, 2, HEADS * N]) for b in range(2)]
        pt = [sb(f"pt{b}", [P, 4, 2, 2, N]) for b in range(2)]
        lnd = sb("lnd", [P, 256])
        rden = [sb(f"rden{b}", [P, 256]) for b in range(2)]
        onrm = [sb(f"onrm{c}", [P, CH]) for c in range(2)]
        prj = [sb(f"prj{c}", [P, CH]) for c in range(2)]
        tt = [sb(f"tt{b}", [P, LT]) for b in range(4)]
        sq2 = [sb(f"sqb{c}", [P, CH]) for c in range(2)]
        xd = [sb(f"xd{b}", [P, 2, LT]) for b in range(2)]
        lg = sb("lg", [P, CH])
        st_ = sb("st_", [P, 4, 4, 2])
        mq = sb("mq", [P, 4, 2, 2])
        vr = sb("vr", [P, 16])
        lnr = sb("lnr", [P, 16])
        rs = sb("rs", [P, 16])
        Lr = sb("Lr", [P, 16, E])
        Ls = sb("Ls", [P, 16, E])
        L = sb("L", [P, 16, E])
        L2 = sb("L2", [P, 16, E])
        eq = sb("eq", [P, 16, E])
        cand = sb("cand", [P, 16, E])
        oh1 = sb("oh1", [P, 16, E])
        oh2 = sb("oh2", [P, 16, E])
        m1 = sb("m1", [P, 16])
        m2 = sb("m2", [P, 16])
        rk = sb("rk", [P, 16])
        dl = sb("dl", [P, 16])
        ed = sb("ed", [P, 16])
        es = sb("es", [P, 16])
        g1 = sb("g1", [P, 16])
        g2 = sb("g2", [P, 16])
        ga = sb("ga", [P, 16, E])
        gb = sb("gb", [P, 16, E])
        gr = sb("gr", [P, 2, 16, E])
        gs = sb("gs", [P, 2, 16, E])
        gp = sb("gp", [P, 8, 8, 16], BF16)
        gT = [sb(f"gT{b}", [P, LT], BF16) for b in range(2)]
        z = [sb(f"z{b}", [P, CH]) for b in range(2)]
        ob = [sb(f"ob{b}", [P, LT]) for b in range(2)]

        bank = ctx.enter_context(nc.psum_tensor("bank", [P, 8, 512], F32))
        S_BANK, PT_BANK, OD_BANK, PRE, G_BANK, Y_BANK = (0, 1), 2, 3, 4, (5, 6), 7

        def cv(name, rows=P):
            return cst[0:rows, CONSTS[name][0]:CONSTS[name][1]]

        def windows(t, c):
            v = t[:, :].rearrange("p (r w k) -> p w r k", r=WS, k=WS)
            return v[:, c * (NW // 2):(c + 1) * (NW // 2)]

        def as_windows(ap):
            return ap.rearrange("p (w r k) -> p w r k", r=WS, k=WS)

        def chunk(t, c):
            return t[:, c * (NW // 2):(c + 1) * (NW // 2), :].rearrange("p w n -> p (w n)")

        def dup(ap):
            return ap.unsqueeze(1).broadcast_to([P, 2, ap.shape[1]])

        pre_bf = bank[:, PRE, :].bitcast(BF16)
        wraw = tt[2][:, 0:NWEIGHT]
        select_raw = tt[3][:, :]
        rel_int = kex[1][:, :, :, :].rearrange("p w h n -> p (w h n)").bitcast(I32)
        onehot = [xd[half][:, :, :].rearrange("p a t -> p (a t)").bitcast(BF16).rearrange("p (k q) -> p k q", q=N)
                  for half in range(2)]

        loaded = sem("loaded")
        late_loaded = sem("late_loaded")
        zeroed = sem("zeroed")
        centred = sem("centred")
        weights_ready = sem("weights_ready")
        onehot_ready = sem("onehot_ready")
        bias_full, bias_high, bias_ready = sem("bias_full"), sem("bias_high"), sem("bias_ready")
        split = sem("split")
        rel_loaded = sem("rel_loaded")
        x_loaded = [sem(f"x_loaded{b}") for b in range(4)]
        xd_loaded = [sem(f"xd_loaded{b}") for b in range(2)]
        stored = [sem(f"stored{b}") for b in range(2)]
        sq_ready, stats_full, msq_ready, var_done, var_ready = (sem("sq_ready"), sem("stats_full"), sem("msq_ready"),
                                                                sem("var_done"), sem("var_ready"))
        ln_done, rstd_done, high_ready, low_ready = sem("ln_done"), sem("rstd_done"), sem("high_ready"), sem("low_ready")
        spread_full, xr_ready = sem("spread_full"), sem("xr_ready")
        q_full, k_full, v_full = sem("q_full"), sem("k_full"), sem("v_full")
        kr_ready = sem("kr_ready")
        q_ready, k_ready, v_ready = sem("q_ready"), sem("k_ready"), sem("v_ready")
        s_full, max_done, shift_done, exp_done = sem("s_full"), sem("max_done"), sem("shift_done"), sem("exp_done")
        t_full, pt_ready, od_full, lnd_done, rden_ready, o_ready = (sem("t_full"), sem("pt_ready"), sem("od_full"),
                                                                  sem("lnd_done"), sem("rden_ready"), sem("o_ready"))
        prj_full, prj_ready, t_ready = sem("prj_full"), sem("prj_ready"), sem("t_ready")
        sq2_ready, stat_ready, lnr_done, rs_ready = sem("sq2_ready"), sem("stat_ready"), sem("lnr_done"), sem("rs_ready")
        lg_full, lg_ready, lgt_full, L_ready = sem("lg_full"), sem("lg_ready"), sem("lgt_full"), sem("L_ready")
        top, delta_ready, ed_ready, g_ready = sem("top"), sem("delta_ready"), sem("ed_ready"), sem("g_ready")
        gate, gp_ready, gt_full, gt_ready = sem("gate"), sem("gp_ready"), sem("gt_full"), sem("gt_ready")
        g_full, z_ready, e_done, y_ready = sem("g_full"), sem("z_ready"), sem("e_done"), sem("y_ready")

        TOP = 16
        BIAS_PARTS = 8
        GATE = 10

        ROUNDS = [("stats", 1, var_done, 1, 1), ("K1", 0, kr_ready, 2, 2), ("V1", 0, v_ready, 8, 8),
                  ("proj1", -1, prj_ready, 2, 2), ("spread0", 1, xr_ready, 2, 1), ("spread1", 1, xr_ready, 2, 2),
                  ("router", -1, lg_ready, 1, 1), ("lgT", -1, L_ready, 2, 2), ("Q0", 1, q_ready, 4, 2),
                  ("K0", 1, kr_ready, 2, 1), ("proj0", 0, prj_ready, 2, 1), ("Q1", 1, q_ready, 4, 4),
                  ("V0", 1, v_ready, 8, 4), ("gT", -1, gt_ready, 1, 1)]
        NAMES = [r[0] for r in ROUNDS]

        class Step:

            def __init__(self, c, n, inner):
                self.c, self.n, self.inner = c, n, inner

            def strip(self, off):
                return Strip(self.c + off, self.n, self.inner)

        class Strip:

            def __init__(self, c, n, inner):
                self.c, self.n, self.inner = c, n, inner
                self.on = inner or 0 <= c < STRIPS

            def buf(self, k):
                return self.c % k

            def count(self, per, k, lag=0):
                v = per * (self.c - lag) + k
                return v + per * U * self.n if self.inner else v

            def rounds(self, k, of):
                v = of * (self.c // k)
                return v + of * (U // k) * self.n if self.inner else v

        def wait(eng, s, value):
            if isinstance(value, int) and value <= 0:
                return
            eng.wait_ge(s, value)

        def steps(run):
            first, last = -1, STRIPS + 1
            lo = 6
            n = (STRIPS - 1 - lo) // U
            for i in range(first, lo):
                run(Step(i, 0, False))
            with nc.Fori(0, n, engines=(run.engine,)) as r:
                for v in range(U):
                    run(Step(lo + v, r, True))
            for i in range(lo + n * U, last + 1):
                run(Step(i, 0, False))

        def stepped(engine_type):
            def mark(f):
                class Run:
                    engine = engine_type

                    def __call__(self, st):
                        f(st)
                steps(Run())
            return mark

        block = ctx.enter_context(nc.Block())
        ET = mybir.EngineType

        @block.sync
        def _(sp):
            for dst, src in ((cst[:, :], consts), (wraw, weights), (sml[:, :], small),
                             (tbraw[:, :, :].rearrange("p a h -> p (a h)"), table)):
                sp.dma_start(dst, src).then_inc(loaded, 16)

            def place(rows, strip):
                pr = strip.buf(PAIRS)
                return rows[pr * P:(pr + 1) * P, bass.ds(strip.rounds(PAIRS, LT), LT)]

            def load(strip):
                src = place(x_rows, strip)
                used = strip.count(2, 2, lag=4)
                wait(sp, t_ready, used)
                sp.dma_start(xs[strip.buf(4)][:, :], src).then_inc(x_loaded[strip.buf(4)], 16)

            load(Strip(0, 0, False))
            sp.dma_start(rel_int, rel.rearrange("k q -> (k q)").partition_broadcast(P)).then_inc(rel_loaded, 16)
            for dst, src in ((wproj[:, :], proj), (rbias[:, :], router_bias), (ebraw[:, :], expert_bias),
                             (select_raw, select_host)):
                sp.dma_start(dst, src).then_inc(late_loaded, 16)

            @stepped(ET.SP)
            def _(st):
                nx = st.strip(2)
                if nx.on:
                    load(nx)
                r = st.strip(-1)
                if r.on:
                    wait(sp, t_ready, r.count(2, 2))
                    for a in range(2):
                        for d in range(2):
                            sp.dma_start(xd[r.buf(2)][64 * d:64 * d + 64, a, :],
                                         tt[r.buf(4)][64 * a:64 * a + 64, :]).then_inc(xd_loaded[r.buf(2)], 16)
                m = st.strip(-2)
                if m.on:
                    dst, summed = place(out_rows, m), m.count(2, 2)
                    wait(sp, y_ready, summed)
                    sp.dma_start(dst, ob[m.buf(2)][:, :]).then_inc(stored[m.buf(2)], 16)

            for b in range(2):
                sp.wait_ge(stored[b], 16 * (STRIPS // 2))

        @block.tensor
        def _(pe):
            mm = nc.tensor.matmul
            pe.wait_ge(loaded, 64)
            mm(bank[:, 0, 0:WR], cv("centre"), wraw[:, 0:WR], start=True, stop=True)
            mm(bank[:, 1, 0:NWEIGHT - WR], cv("centre"), wraw[:, WR:NWEIGHT], start=True, stop=True).then_inc(centred, 1)

            def bias_rows(n):
                if n == 0:
                    pe.wait_ge(onehot_ready, 2)
                for k in range(n * N // BIAS_PARTS, (n + 1) * N // BIAS_PARTS):
                    for q in (0, N):
                        dst = bank[q:q + N, 2 + k // 32, 12 * (k % 32):12 * (k % 32) + 12]
                        for half in range(2):
                            last = mm(dst, onehot[half][:, k, :], tb[:, half, :, :].rearrange("p s h -> p (s h)"),
                                      start=(half == 0), stop=(half == 1), skip_group_check=True)
                if n == BIAS_PARTS - 1:
                    last.then_inc(bias_full, 1)

            def pre_free(st, name):
                at, c = NAMES.index(name), st.c
                while True:
                    at -= 1
                    if at < 0:
                        at, c = len(ROUNDS) - 1, c - 1
                    if c < -1:
                        return
                    _, off, s, per, k = ROUNDS[at]
                    if st.inner or 0 <= c + off < STRIPS:
                        wait(pe, s, Strip(c + off, st.n, st.inner).count(per, k))
                        return

            def scores(st, u):
                s = st.strip(0)
                b = bank[:, S_BANK[u % 2], :]
                if u % 4 == 0:
                    pe.wait_ge(q_ready, s.count(4, 2 * (u // 4) + 2))
                    pe.wait_ge(k_ready, s.count(2, u // 4 + 1))
                wait(pe, shift_done, s.count(UNITS, u - 1))
                mm(b, tile_id[:, :], dup(bias_hl[:, :, :].rearrange("p h k -> p (h k)")), start=True, stop=False,
                   skip_group_check=True)
                for j in range(2):
                    w = 2 * u + j
                    last = mm(b[:, 256 * j:256 * j + 256], qbd[s.buf(2)][:, w, :, :].rearrange("p a q -> p (a q)"),
                              kex[s.buf(2)][:, w, :, :].rearrange("p h k -> p (h k)"), start=False, stop=(j == 1),
                              skip_group_check=True)
                last.then_inc(s_full, 1)

            def transposes(s, u):
                pe.wait_ge(exp_done, s.count(UNITS, u + 1))
                wait(pe, pt_ready, s.count(UNITS, u))
                for j in range(4):
                    last = nc.tensor.transpose(bank[:, PT_BANK, 128 * j:128 * j + 128],
                                               probs[u % 2][:, j // 2, 128 * (j % 2):128 * (j % 2) + 128], cv("ident"))
                last.then_inc(t_full, 1)

            def values(s, u):
                g = u // 2
                pe.wait_ge(pt_ready, s.count(UNITS, u + 1))
                if u % 2 == 0:
                    pe.wait_ge(v_ready, s.count(8, 4 * (g // 2) + 4))
                    wait(pe, o_ready, s.count(GROUPS, g))
                for wl in range(2):
                    w4 = 2 * (u % 2) + wl
                    for a in range(2):
                        for j in range(2):
                            q = 64 * a + 32 * j
                            last = mm(bank[q:q + 32, OD_BANK, N * w4:N * w4 + N], vbd[s.buf(2)][:, 2 * u + wl, q:q + 32],
                                      pt[g % 2][:, w4, j, a, :], start=True, stop=True, skip_group_check=True)
                if u % 2 == 1:
                    for a in range(2):
                        for j in range(2):
                            q = 64 * a + 32 * j
                            last = mm(bank[q:q + 32, OD_BANK, 256:512], cv("pair"), pt[g % 2][:, :, j, a, :],
                                      start=True, stop=True, skip_group_check=True)
                    last.then_inc(od_full, 1)

            def project(st, s, c, name):
                pe.wait_ge(o_ready, s.count(GROUPS, 2 * c + 2))
                pre_free(st, name)
                mm(bank[:, PRE, :], wproj[:, :], onrm[c][:, :], start=True, stop=True).then_inc(prj_full, 1)

            def channel_sums(st, s):
                pe.wait_ge(x_loaded[s.buf(4)], s.rounds(4, 16) + 16)
                pre_free(st, "stats")
                for c in range(2):
                    mm(bank[32 * c:32 * c + 32, PRE, :], cv("stat"), windows(xs[s.buf(4)], c), start=True, stop=True)
                pe.wait_ge(sq_ready, s.count(2, 2))
                for c in range(2):
                    last = mm(bank[64 + 32 * c:96 + 32 * c, PRE, :], cv("stat"), sq[c][:, :], start=True, stop=True)
                last.then_inc(stats_full, 1)

            def router(st, s):
                pe.wait_ge(t_ready, s.count(2, 2))
                pe.wait_ge(sq2_ready, s.count(2, 2))
                pre_free(st, "router")
                for c in range(2):
                    mm(bank[32 * c:32 * c + 32, PRE, :], wcen[:, WR:WR + 32],
                       tt[s.buf(4)][:, c * CH:(c + 1) * CH], start=True, stop=True)
                for c in range(2):
                    last = mm(bank[64 + 32 * c:96 + 32 * c, PRE, :], cv("stat"), sq2[c][:, :], start=True, stop=True)
                last.then_inc(lg_full, 1)

            def transpose_logits(st, s):
                pe.wait_ge(lg_ready, s.count(1, 1))
                pre_free(st, "lgT")
                for ttl in range(4):
                    last = nc.tensor.transpose(bank[:, PRE, 128 * ttl:128 * ttl + 128],
                                               lg[:, 128 * ttl:128 * ttl + 128], cv("ident"))
                last.then_inc(lgt_full, 1)

            def transpose_gates(st, s):
                pe.wait_ge(gp_ready, s.count(1, 1))
                pre_free(st, "gT")
                for t8 in range(8):
                    ttl, c = t8 // 2, t8 % 2
                    last = nc.tensor.transpose(pre_bf[:, c * CH + 128 * ttl:c * CH + 128 * ttl + 128],
                                               gp[:, t8, :, :].rearrange("p s e -> p (s e)"), ident_bf[:, :])
                last.then_inc(gt_full, 1)

            def queries(st, s, c):
                pe.wait_ge(xr_ready, s.count(2, c + 1))
                pre_free(st, f"Q{c}")
                mm(bank[:, PRE, :], wcen[:, WQ:WQ + P], chunk(xr[s.buf(2)], c), start=True, stop=True).then_inc(q_full, 1)

            def keys(st, s, c):
                pre_free(st, f"K{c}")
                mm(bank[:, PRE, :], wcen[:, WK:WK + P], chunk(xr[s.buf(2)], c), start=True, stop=True).then_inc(k_full, 1)

            def spread_std(st, s, c):
                if s.c == 0 and c == 0 and not s.inner:
                    pe.wait_ge(weights_ready, 1)
                if c == 0:
                    pe.wait_ge(high_ready, s.count(1, 1))
                    pe.wait_ge(low_ready, s.count(1, 1))
                pre_free(st, f"spread{c}")
                mm(bank[:, PRE, :], spread[:, c, :], var_hl[:, :], start=True, stop=True).then_inc(spread_full, 1)

            def value_rows(st, s, c):
                pre_free(st, f"V{c}")
                for pair in range(4):
                    w = 8 * c + 2 * pair
                    last = mm(bank[:, PRE, 128 * pair:128 * pair + 128],
                              xr[s.buf(2)][:, w:w + 2, :].rearrange("p w n -> p (w n)"),
                              wcen[:, WV:WV + P], start=True, stop=True)
                last.then_inc(v_full, 1)

            def gates_wide(s, n):
                c, j, a = n // 8, n % 8 // 2, n % 2
                if n == 0:
                    pe.wait_ge(gt_ready, s.count(1, 1))
                wait(pe, z_ready, s.count(ITEMS, n - 1))
                mm(bank[:, G_BANK[n % 2], :], select[:, 4 * a + j, :], gT[s.buf(2)][:, c * CH:(c + 1) * CH],
                   start=True, stop=True).then_inc(g_full, 1)

            def experts(s, n):
                c, j, a = n // 8, n % 8 // 2, n % 2
                if n % 8 == 0:
                    wait(pe, y_ready, s.count(2, c))
                    for k in range(2):
                        mm(bank[:, Y_BANK, :], eb[:, k, :], gT[s.buf(2)][:, c * CH:(c + 1) * CH],
                           start=(k == 0), stop=False, skip_group_check=True)
                pe.wait_ge(z_ready, s.count(ITEMS, n + 1))
                mm(bank[64 * a:64 * a + 64, Y_BANK, :], wcen[:, WE + C * j:WE + C * j + C], z[n % 2][:, :],
                   start=False, stop=(j == 3), skip_group_check=True).then_inc(e_done, 1)

            @stepped(ET.PE)
            def _(st):
                pre, att, old, moe = st.strip(1), st.strip(0), st.strip(-1), st.strip(-2)
                first = st.c < 0
                if st.c == 0:
                    pe.wait_ge(bias_ready, 1)
                for k in range(SLOTS):
                    if first and 5 <= k < 5 + BIAS_PARTS:
                        bias_rows(k - 5)
                    if k and k % 2 == 0:
                        if moe.on:
                            gates_wide(moe, k + 1)
                        if k == 2 and att.on:
                            keys(st, att, 1)
                        if k == 6 and pre.on:
                            spread_std(st, pre, 1)
                        if k == 8 and old.on:
                            transpose_logits(st, old)
                        if k == 4 and old.on:
                            project(st, old, 1, "proj1")
                        if k == 12 and att.on:
                            project(st, att, 0, "proj0")
                    if k == 0 and old.on:
                        transposes(old, 7)
                    if k % 2 == 0 and att.on:
                        if k:
                            transposes(att, k // 2 - 1)
                        scores(st, k // 2)
                    if k == 1 and pre.on:
                        channel_sums(st, pre)
                    if k == 3 and att.on:
                        value_rows(st, att, 1)
                    if k == 14 and pre.on:
                        value_rows(st, pre, 0)
                    if k == 7 and old.on:
                        router(st, old)
                    if k == 10 and pre.on:
                        keys(st, pre, 0)
                    if k == 1 and old.on:
                        values(old, 7)
                    if moe.on:
                        if k == 0:
                            gates_wide(moe, 0)
                            gates_wide(moe, 1)
                        if k % 2 == 1:
                            if k < SLOTS - 1:
                                gates_wide(moe, k + 1)
                            experts(moe, k - 1)
                            experts(moe, k)
                    if k == 5 and pre.on:
                        spread_std(st, pre, 0)
                    if k in (9, 13) and pre.on:
                        queries(st, pre, (k - 9) // 4)
                    if k % 2 == 1 and k >= 3 and att.on:
                        values(att, (k - 3) // 2)
                    if k == 15 and old.on:
                        transpose_gates(st, old)

        @block.scalar
        def _(act):
            af = nc.scalar.activation
            nc.scalar.preload_act_table_set("natural_log_exp_and_others")
            act.wait_ge(loaded, 64)

            def exps(s, u):
                act.wait_ge(shift_done, s.count(UNITS, u + 1))
                wait(act, t_full, s.count(UNITS, u - 1))
                af(probs[u % 2][:, :, :].rearrange("p w k -> p (w k)"),
                   shifted[u % 2][:, :, :].rearrange("p g k -> p (g k)"), ACT.Exp).then_inc(exp_done, 1)

            def move_pt(s, u):
                g = u // 2
                act.wait_ge(t_full, s.count(UNITS, u + 1))
                if u % 2 == 0:
                    wait(act, od_full, s.count(GROUPS, g - 1))
                af(pt[g % 2][:, 2 * (u % 2):2 * (u % 2) + 2, :, :, :].rearrange("p w j a q -> p (w j a q)"),
                   bank[:, PT_BANK, :], ACT.Copy).then_inc(pt_ready, 1)

            def inverse_sums(s, g):
                act.wait_ge(od_full, s.count(GROUPS, g + 1))
                wait(act, rden_ready, s.count(GROUPS, g))
                af(lnd[:, :], bank[:, OD_BANK, 256:512], ACT.Ln).then_inc(lnd_done, 1)
                act.wait_ge(lnd_done, s.count(GROUPS, g + 1))
                wait(act, o_ready, s.count(GROUPS, g - 1))
                af(rden[g % 2][:, :], lnd[:, :], ACT.Exp, scale=-1.0).then_inc(rden_ready, 1)

            def square(s, c):
                if c == 0:
                    act.wait_ge(x_loaded[s.buf(4)], s.rounds(4, 16) + 16)
                    wait(act, stats_full, s.count(1, 1, lag=1))
                af(as_windows(sq[c][:, :]), windows(xs[s.buf(4)], c), ACT.Square).then_inc(sq_ready, 1)

            def square_mean(s):
                act.wait_ge(stats_full, s.count(1, 1))
                af(msq[64:128, :], bank[0:64, PRE, :], ACT.Square).then_inc(msq_ready, 1)

            def inverse_std(s):
                act.wait_ge(var_ready, s.count(1, 1))
                af(msq[64:128, :], var[64:128, :], ACT.Ln, bias=sml[64:128, 2:3]).then_inc(ln_done, 1)
                act.wait_ge(ln_done, s.count(1, 1))
                af(var[64:128, :], msq[64:128, :], ACT.Exp, scale=-0.5).then_inc(rstd_done, 1)

            def high_part(s):
                act.wait_ge(rstd_done, s.count(1, 1))
                wait(act, spread_full, s.count(2, 2, lag=1))
                af(var_hl[64:128, :], var[64:128, :], ACT.Copy).then_inc(high_ready, 1)

            def move_k(s, c):
                act.wait_ge(k_full, s.count(2, c + 1))
                wait(act, k_ready, s.count(2, c))
                af(kr[:, :], bank[:, PRE, :], ACT.Copy).then_inc(kr_ready, 1)

            def move_v(s, c):
                act.wait_ge(v_full, s.count(2, c + 1))
                wait(act, od_full, s.count(GROUPS, GROUPS, lag=2))
                for wp in range(2):
                    src = bank[64 * wp:64 * wp + 64, PRE, :].rearrange("p (w m h d) -> p w m h d", w=4, h=2, d=HD)
                    for h in range(2):
                        dst = vbd[s.buf(2)][64 * h:64 * h + 64, 8 * c + wp:8 * c + 8:2, :].rearrange(
                            "p w (m h d) -> p w m h d", h=2, d=HD)
                        af(dst[:, :, :, h, :], src[:, :, :, h, :], ACT.Copy).then_inc(v_ready, 1)

            def square_residual(s, c):
                act.wait_ge(t_ready, s.count(2, c + 1))
                wait(act, lg_full, s.count(1, 1, lag=1))
                af(sq2[c][:, :], tt[s.buf(4)][:, c * CH:(c + 1) * CH], ACT.Square).then_inc(sq2_ready, 1)

            def move_proj(s, c):
                act.wait_ge(prj_full, s.count(2, c + 1))
                wait(act, t_ready, s.count(2, c + 1, lag=1))
                af(prj[c][:, :], bank[:, PRE, :], ACT.Identity, bias=sml[:, 0:1]).then_inc(prj_ready, 1)

            @stepped(ET.Activation)
            def _(st):
                pre, att, old = st.strip(1), st.strip(0), st.strip(-1)
                for k in range(SLOTS):
                    if k == 0 and pre.on:
                        square(pre, 0)
                        square(pre, 1)
                    if k == 1 and pre.on:
                        square_mean(pre)
                    if k == 9 and old.on:
                        act.wait_ge(stat_ready, old.count(1, 1))
                        af(lnr[:, :], vr[:, :], ACT.Ln).then_inc(lnr_done, 1)
                        act.wait_ge(lnr_done, old.count(1, 1))
                        wait(act, gp_ready, old.count(1, 1, lag=1))
                        af(rs[:, :], lnr[:, :], ACT.Exp, scale=-0.5).then_inc(rs_ready, 1)
                    if k == 3 and att.on:
                        move_v(att, 1)
                    if k % 2 == 1 and att.on:
                        exps(att, k // 2)
                    if k == 1 and pre.on:
                        inverse_std(pre)
                    if k == 2 and att.on:
                        move_k(att, 1)
                    if k == 2 and old.on:
                        inverse_sums(old, 3)
                    if k == 2 and pre.on:
                        high_part(pre)
                    if k % 4 == 2 and k >= 6 and att.on:
                        inverse_sums(att, (k - 6) // 4)
                    if k == 12 and old.on:
                        act.wait_ge(delta_ready, old.count(1, 1))
                        af(ed[:, :], dl[:, :], ACT.Exp).then_inc(ed_ready, 1)
                    if k == 4 and old.on:
                        move_proj(old, 1)
                    if k == 0 and old.on:
                        move_pt(old, 7)
                    if k % 2 == 0 and k >= 2 and att.on:
                        move_pt(att, k // 2 - 1)
                    if k == 12 and att.on:
                        move_proj(att, 0)
                    if k == 5 and old.on:
                        square_residual(old, 1)
                    if k == 7 and old.on:
                        act.wait_ge(lg_full, old.count(1, 1))
                        wait(act, lgt_full, old.count(1, 1, lag=1))
                        af(lg[:, :], bank[:, PRE, :], ACT.Copy).then_inc(lg_ready, 1)
                    if k in (9, 13) and pre.on:
                        c = (k - 9) // 4
                        act.wait_ge(q_full, pre.count(2, c + 1))
                        wait(act, s_full, pre.count(UNITS, UNITS, lag=2))
                        for a in range(2):
                            af(qbd[pre.buf(2)][64 * a:64 * a + 64, 8 * c:8 * c + 8, a, :],
                               bank[64 * a:64 * a + 64, PRE, :].rearrange("p (w q) -> p w q", q=N), ACT.Copy,
                               scale=float(HD) ** -0.5).then_inc(q_ready, 1)
                    if k == 3 and old.on:
                        square_residual(old, 0)
                    if k == 14 and pre.on:
                        move_v(pre, 0)
                    if k == 10 and pre.on:
                        move_k(pre, 0)

        @block.gpsimd
        def _(pool):
            tt_ = nc.gpsimd.tensor_tensor
            for b in range(2):
                nc.gpsimd.memset(qbd[b][:, :, :, :], 0.0).then_inc(zeroed, 1)
                nc.gpsimd.memset(vbd[b][:, :, :], 0.0).then_inc(zeroed, 1)

            @stepped(ET.Pool)
            def _(st):
                pre, att, old, moe = st.strip(1), st.strip(0), st.strip(-1), st.strip(-2)

                def residual(s, c):
                    pool.wait_ge(prj_ready, s.count(2, c + 1))
                    wait(pool, y_ready, s.count(2, c + 1, lag=4))
                    if c == 1:
                        wait(pool, z_ready, s.count(ITEMS, ITEMS, lag=2))
                    tt_(as_windows(tt[s.buf(4)][:, c * CH:(c + 1) * CH]), as_windows(prj[c][:, :]),
                        windows(xs[s.buf(4)], c), op=ALU.add).then_inc(t_ready, 1)

                if old.on:
                    residual(old, 1)
                if old.on:
                    wide = lambda ap: ap.unsqueeze(2).broadcast_to([P, 16, E])
                    part = lambda n: gp[:, :, 2 * n:2 * n + 2, :].rearrange("p t q m -> p q t m")
                    v4 = lambda t: t[:, :, :, :].rearrange("p q (t a) e -> p q t (a e)", a=2)
                    v3 = lambda ap: ap.rearrange("p (t a) e -> p t (a e)", a=2)
                    pool.wait_ge(g_ready, old.count(2, 2))
                    wait(pool, gt_full, old.count(1, 1, lag=1))
                    tt_(ga[:, :, :], oh1[:, :, :], wide(g1[:, :]), op=ALU.mult).then_inc(gate, 1)
                    tt_(gb[:, :, :], oh2[:, :, :], wide(g2[:, :]), op=ALU.mult).then_inc(gate, 1)
                    pool.wait_ge(gate, old.count(GATE, 2))
                    tt_(gr[:, 0, :, :], ga[:, :, :], gb[:, :, :], op=ALU.add).then_inc(gate, 1)
                    tt_(gp[:, :, 0, :], v3(ga[:, :, :]), v3(gb[:, :, :]), op=ALU.add).then_inc(gate, 1)
                    tt_(gp[:, :, 6, :], v3(ga[:, :, :]), v3(gb[:, :, :]), op=ALU.add).then_inc(gate, 1)
                    pool.wait_ge(rs_ready, old.count(1, 1))
                    pool.wait_ge(gate, old.count(GATE, 3))
                    tt_(gr[:, 1, :, :], gr[:, 0, :, :], wide(rs[:, :]), op=ALU.mult).then_inc(gate, 1)
                    tt_(gp[:, :, 1, :].rearrange("p t (a e) -> p t a e", a=2),
                        gr[:, 0, :, :].rearrange("p (t a) e -> p t a e", a=2),
                        rs[:, :].rearrange("p (t a) -> p t a", a=2).unsqueeze(3).broadcast_to([P, 8, 2, E]),
                        op=ALU.mult).then_inc(gate, 1)
                    pool.wait_ge(gate, old.count(GATE, 7))
                    tt_(v4(gs), v4(gr), part(0), op=ALU.subtract).then_inc(gate, 1)
                    tt_(part(1), v4(gr), part(0), op=ALU.subtract).then_inc(gate, 1)
                    tt_(gp[:, :, 7, :], v3(gr[:, 0, :, :]), gp[:, :, 0, :], op=ALU.subtract).then_inc(gate, 1)
                    pool.wait_ge(gate, old.count(GATE, GATE))
                    tt_(part(2), v4(gs), part(1), op=ALU.subtract).then_inc(gp_ready, 1)
                if att.on:
                    residual(att, 0)

        @block.vector
        def _(dve):
            tt_, red = nc.vector.tensor_tensor, nc.vector.tensor_reduce
            copy = nc.vector.tensor_copy
            dve.wait_ge(loaded, 64)

            def split_step(ins, n):
                ins.then_inc(split, 1)
                dve.wait_ge(split, n)

            split_step(copy(tb[:, :, 0, :], tbraw[:, :, :]), 1)
            split_step(tt_(tbres[:, :, :], tbraw[:, :, :], tb[:, :, 0, :], op=ALU.subtract), 2)
            split_step(copy(tb[:, :, 1, :], tbres[:, :, :]), 3)
            tt_(tb[:, :, 2, :], tbres[:, :, :], tb[:, :, 1, :], op=ALU.subtract)
            dve.wait_ge(centred, 1)
            dve.wait_ge(zeroed, 4)
            copy(wcen[:, 0:WR], bank[:, 0, 0:WR])
            tt_(wcen[:, WR:WR + 32], bank[:, 1, 0:32], cv("stat"), op=ALU.add)
            copy(wcen[:, WE:NWEIGHT], bank[:, 1, 32:NWEIGHT - WR])
            copy(spread[:, :, :].rearrange("p c n -> p (c n)"), cv("spread")).then_inc(weights_ready, 1)
            dve.wait_ge(rel_loaded, 16)
            for half in range(2):
                nc.vector.tensor_scalar(onehot[half].rearrange("p k q -> p (k q)"), rel_int,
                                        cv("row")[:, half:half + 1], None, ALU.is_equal).then_inc(onehot_ready, 1)

            def late_setup():
                dve.wait_ge(late_loaded, 64)
                copy(tile_id[:, :], cv("tile"))
                copy(ident_bf[:, :], cv("ident"))
                copy(select[:, :, :].rearrange("p s n -> p (s n)"), select_raw)
                split_step(copy(eb[:, 0, :], ebraw[:, :]), 4)
                split_step(tt_(ebres[:, :], ebraw[:, :], eb[:, 0, :], op=ALU.subtract), 5)
                split_step(copy(ebmid[:, :], ebres[:, :]), 6)
                copy(eb[96:128, 0, :], ebmid[96:128, :])
                copy(eb[64:96, 1, :], ebmid[64:96, :])
                nc.vector.memset(eb[96:128, 1, :], 0.0)
                tt_(eb[0:64, 1, :], ebres[0:64, :], ebmid[0:64, :], op=ALU.subtract)
                dve.wait_ge(bias_full, 1)
                for kh in range(2):
                    dst = bias[:, :, 32 * kh:32 * kh + 32]
                    src = bank[:, 2 + kh, 0:384].rearrange("p (k s h) -> p s h k", s=PARTS, h=HEADS)
                    split_step(copy(dst, src[:, 2, :, :]), 7 + 3 * kh)
                    for n, part in enumerate((1, 0)):
                        split_step(tt_(dst, dst, src[:, part, :, :], op=ALU.add), 8 + 3 * kh + n)
                copy(bias_hl[:, :, :], bias[:, :, :]).then_inc(bias_high, 1)
                dve.wait_ge(bias_high, 1)
                tt_(bias_hl[64:128, :, :], bias[64:128, :, :], bias_hl[64:128, :, :].bitcast(F32),
                    op=ALU.subtract).then_inc(bias_ready, 1)

            def softmax_shift(s, u):
                b = bank[:, S_BANK[u % 2], :].rearrange("p (g k) -> p g k", k=N)
                dve.wait_ge(s_full, s.count(UNITS, u + 1))
                red(mx[u % 2][:, :], b, axis=AX_X, op=ALU.max).then_inc(max_done, 1)
                dve.wait_ge(max_done, s.count(UNITS, u + 1))
                wait(dve, exp_done, s.count(UNITS, u - 1))
                tt_(shifted[u % 2][:, :, :], b, mx[u % 2][:, :].unsqueeze(2).broadcast_to([P, 8, N]),
                    op=ALU.subtract).then_inc(shift_done, 1)

            def normalise(s, g):
                dve.wait_ge(rden_ready, s.count(GROUPS, g + 1))
                c = g // 2
                wait(dve, prj_full, s.count(2, c + 1, lag=1))
                tt_(onrm[c][:, 256 * (g % 2):256 * (g % 2) + 256], bank[:, OD_BANK, 0:256], rden[g % 2][:, :],
                    op=ALU.mult).then_inc(o_ready, 1)

            def gated(s, n):
                c, a = n // 8, n % 2
                dve.wait_ge(g_full, s.count(ITEMS, n + 1))
                if n == 0:
                    dve.wait_ge(xd_loaded[s.buf(2)], s.rounds(2, 64) + 64)
                wait(dve, e_done, s.count(ITEMS, n - 1))
                tt_(z[n % 2][:, :], bank[:, G_BANK[n % 2], :], xd[s.buf(2)][:, a, c * CH:(c + 1) * CH],
                    op=ALU.mult).then_inc(z_ready, 1)

            def finish(s, c):
                dve.wait_ge(e_done, s.count(ITEMS, 8 * c + 8))
                if c == 0:
                    wait(dve, stored[s.buf(2)], s.rounds(2, 16))
                tt_(windows(ob[s.buf(2)], c), as_windows(bank[:, Y_BANK, :]),
                    as_windows(tt[s.buf(4)][:, c * CH:(c + 1) * CH]), op=ALU.add).then_inc(y_ready, 1)

            def top_step(s, n, ins):
                ins.then_inc(top, 1)
                dve.wait_ge(top, s.count(TOP, n))

            wide = lambda ap: ap.unsqueeze(2).broadcast_to([P, 16, E])

            def pick(s, n, vals, m, oh):
                order = cv("order").unsqueeze(1).broadcast_to([P, 16, E])
                top_step(s, n + 1, red(m[:, :], vals[:, :, :], axis=AX_X, op=ALU.max))
                top_step(s, n + 2, tt_(eq[:, :, :], vals[:, :, :], wide(m[:, :]), op=ALU.is_equal))
                top_step(s, n + 3, tt_(cand[:, :, :], eq[:, :, :], order, op=ALU.mult))
                top_step(s, n + 4, red(rk[:, :], cand[:, :, :], axis=AX_X, op=ALU.max))
                top_step(s, n + 5, tt_(oh[:, :, :], cand[:, :, :], wide(rk[:, :]), op=ALU.is_equal))

            def token_statistics(s):
                dve.wait_ge(lgt_full, s.count(1, 1))
                src = bank[:, PRE, :].rearrange("p (t c m) -> p t c m", t=4, m=32)
                copy(Lr[:, :, :].rearrange("p (t c a) e -> p t c (a e)", a=2, c=2),
                     src[:, :, 0:2, 0:16]).then_inc(L_ready, 1)
                copy(st_[:, :, :, :], src[:, :, :, 16:18]).then_inc(L_ready, 1)
                dve.wait_ge(L_ready, s.count(2, 2))
                top_step(s, 1, tt_(mq[:, :, :, :], st_[:, :, 0:2, :], st_[:, :, 0:2, :], op=ALU.mult))
                top_step(s, 2, tt_(vr[:, :].rearrange("p (t m) -> p t m", m=4),
                                   st_[:, :, 2:4, :].rearrange("p t c a -> p t (c a)"),
                                   mq[:, :, :, :].rearrange("p t c a -> p t (c a)"), op=ALU.subtract))
                nc.vector.tensor_scalar(vr[:, :], vr[:, :], 0.0, 1e-5, ALU.max, ALU.add).then_inc(stat_ready, 1)

            def top_one(s):
                dve.wait_ge(rs_ready, s.count(1, 1))
                top_step(s, 3, tt_(Ls[:, :, :], Lr[:, :, :], wide(rs[:, :]), op=ALU.mult))
                top_step(s, 4, tt_(L[:, :, :].rearrange("p (t a) e -> p t (a e)", a=2),
                                   Ls[:, :, :].rearrange("p (t a) e -> p t (a e)", a=2),
                                   rbias[:, :].unsqueeze(1).broadcast_to([P, 8, 16]), op=ALU.add))
                wait(dve, gp_ready, s.count(1, 1, lag=1))
                pick(s, 4, L, m1, oh1)

            def top_second(s):
                top_step(s, 10, nc.vector.scalar_tensor_tensor(out=L2[:, :, :], in0=oh1[:, :, :], scalar=-BIG,
                                                               in1=L[:, :, :], op0=ALU.mult, op1=ALU.add))
                pick(s, 10, L2, m2, oh2)
                tt_(dl[:, :], m2[:, :], m1[:, :], op=ALU.subtract).then_inc(delta_ready, 1)

            def gates(s):
                dve.wait_ge(ed_ready, s.count(1, 1))
                top_step(s, TOP, nc.vector.tensor_scalar(es[:, :], ed[:, :], 1.0, None, ALU.add))
                nc.vector.reciprocal(g1[:, :], es[:, :]).then_inc(g_ready, 1)
                dve.wait_ge(g_ready, s.count(2, 1))
                tt_(g2[:, :], ed[:, :], g1[:, :], op=ALU.mult).then_inc(g_ready, 1)

            def variance(s):
                dve.wait_ge(msq_ready, s.count(1, 1))
                wait(dve, low_ready, s.count(1, 1, lag=1))
                tt_(var[64:128, :], bank[64:128, PRE, :], msq[64:128, :], op=ALU.subtract).then_inc(var_done, 1)
                dve.wait_ge(var_done, s.count(1, 1))
                nc.vector.tensor_scalar(var[64:128, :], var[64:128, :], 0.0, None, ALU.max).then_inc(var_ready, 1)

            def low_part(s):
                dve.wait_ge(high_ready, s.count(1, 1))
                tt_(var_hl[0:64, :], var[64:128, :], var_hl[64:128, :].bitcast(F32),
                    op=ALU.subtract).then_inc(low_ready, 1)

            def scale_x(s, c):
                dve.wait_ge(spread_full, s.count(2, c + 1))
                if c == 0:
                    dve.wait_ge(x_loaded[s.buf(4)], s.rounds(4, 16) + 16)
                wait(dve, v_full, s.count(2, 2, lag=2))
                wait(dve, k_full, s.count(2, 2, lag=2))
                tt_(as_windows(chunk(xr[s.buf(2)], c)), windows(xs[s.buf(4)], c), as_windows(bank[:, PRE, :]),
                    op=ALU.mult).then_inc(xr_ready, 1)

            def mask_k(s, c, pair):
                if pair == 0:
                    dve.wait_ge(kr_ready, s.count(2, c + 1))
                    wait(dve, s_full, s.count(UNITS, UNITS, lag=2))
                for h in (2 * pair, 2 * pair + 1):
                    last = nc.vector.tensor_scalar(kex[s.buf(2)][:, 8 * c:8 * c + 8, h, :],
                                                   kr[:, :].rearrange("p (w n) -> p w n", n=N),
                                                   cv("head")[:, h:h + 1], None, ALU.mult)
                if pair == 1:
                    last.then_inc(k_ready, 1)

            @stepped(ET.DVE)
            def _(st):
                pre, att, old, moe = st.strip(1), st.strip(0), st.strip(-1), st.strip(-2)
                for k in range(SLOTS):
                    if k % 2 == 0 and k and moe.on:
                        gated(moe, k)
                        gated(moe, k + 1)
                    if k == 6 and pre.on:
                        scale_x(pre, 1)
                    if k == 12 and old.on:
                        gates(old)
                    if k in (6, 10, 14) and att.on:
                        normalise(att, (k - 6) // 4)
                    if k == 8 and old.on:
                        token_statistics(old)
                    if k % 2 == 0 and att.on:
                        softmax_shift(att, k // 2)
                    if k == 0 and moe.on:
                        gated(moe, 0)
                        gated(moe, 1)
                    if k == 1 and pre.on:
                        variance(pre)
                    if k == 2 and old.on:
                        normalise(old, 3)
                    if k == 2 and pre.on:
                        low_part(pre)
                    if k == 5 and pre.on:
                        scale_x(pre, 0)
                    if k == 3 and att.on:
                        mask_k(att, 1, 0)
                        mask_k(att, 1, 1)
                    if k == 7 and moe.on:
                        finish(moe, 0)
                    if k == 13 and pre.on:
                        mask_k(pre, 0, 0)
                        mask_k(pre, 0, 1)
                    if old.on:
                        if k == 9:
                            top_one(old)
                        if k == 11:
                            top_second(old)
                        if k == 15:
                            dve.wait_ge(gt_full, old.count(1, 1))
                            copy(gT[old.buf(2)][:, :], pre_bf[:, :]).then_inc(gt_ready, 1)
                    if k == 15 and moe.on:
                        finish(moe, 1)
                if st.c < 0:
                    late_setup()


def constants(np):
    p = np.arange(P)
    a, ch = p // C, p % C
    same = a[:, None] == a[None, :]
    parts = {
        "centre": np.eye(P) - same / C,
        "spread": np.concatenate([(p[:, None] % 64 == 32 * c + 16 + a[None, :]) for c in range(2)], axis=1),
        "ident": np.eye(P),
        "head": ch[:, None] // HD == np.arange(HEADS)[None, :],
        "pair": p[:, None] // N == np.arange(32)[None, :] // HD,
        "tile": p[:, None] % N == p[None, :] % N,
        "order": np.broadcast_to(np.arange(E, 0, -1), (P, E)),
        "row": p[:, None] + P * np.arange(2)[None, :],
        "stat": (np.arange(32)[None, :] == 16 + a[:, None]) / C,
    }
    c = np.zeros((P, NCONST), np.float32)
    for name, (lo, hi) in CONSTS.items():
        c[:, lo:hi] = parts[name]
    return c


def select_matrix(np):
    p = np.arange(P)
    cols = np.arange(8 * P)
    img, pair, e2 = cols // (4 * P), cols // P % 4, cols % P // C
    return ((p[:, None] % 32 == (16 + 8 * img + 2 * pair + e2)[None, :]) & (p[:, None] < 32 * PARTS)).astype(np.float32)


def kernel(x, L0_conv_w_qkv, L0_conv_bias_table, L0_conv_w_proj, L0_conv_b_proj, L0_conv_rel_index,
           L0_ffn_router_w, L0_ffn_router_b, L0_ffn_expert_w, L0_ffn_expert_b):
    import numpy as np
    import concourse.bacc as bacc
    from concourse.bass_utils import run_bass_kernel_spmd

    w = np.zeros((P, NWEIGHT), np.float32)
    wproj = np.zeros((P, P), np.float32)
    qkv_t = np.asarray(L0_conv_w_qkv).T
    small = np.zeros((P, 4), np.float32)
    eb = np.zeros((P, P), np.float32)
    for a in range(2):
        r = slice(C * a, C * a + C)
        for i, at in enumerate((WQ, WK, WV)):
            w[r, at + C * a:at + C * a + C] = qkv_t[:, C * i:C * i + C]
        w[r, WR + E * a:WR + E * a + E] = L0_ffn_router_w
        wproj[r, r] = np.asarray(L0_conv_w_proj).T
        small[r, 0] = L0_conv_b_proj
        for s in range(PARTS):
            eb[32 * s + E * a:32 * s + E * a + E, r] = L0_ffn_expert_b
        for s in (96, 112):
            eb[s + E * a:s + E * a + E, r] = L0_ffn_expert_b
    w[:, WE:WE + 4 * C] = np.asarray(L0_ffn_expert_w).reshape(4, P, C).transpose(1, 0, 2).reshape(P, 4 * C)
    small[:, 2] = 1e-6
    router_bias = np.zeros((P, 2 * E), np.float32)
    router_bias[:] = np.tile(np.asarray(L0_ffn_router_b), 2)
    rows = L0_conv_bias_table.shape[0]
    table = np.zeros((2 * P, HEADS), np.float32)
    table[:rows] = L0_conv_bias_table
    table = np.ascontiguousarray(table.reshape(2, P, HEADS).transpose(1, 0, 2).reshape(P, 2 * HEADS))
    arrays = {"x": np.ascontiguousarray(x), "weights": w, "proj": wproj, "small": small, "router_bias": router_bias, "expert_bias": eb,
              "table": table, "rel": np.ascontiguousarray(np.asarray(L0_conv_rel_index).T), "consts": constants(np),
              "select": select_matrix(np)}

    nc = bacc.Bacc("TRN2", target_bir_lowering=False, num_devices=1)
    args = [nc.dram_tensor(f"in_{n}", a.shape, mybir.dt.from_np(a.dtype), kind="ExternalInput").ap()
            for n, a in arrays.items()]
    result = nc.dram_tensor("out_0", x.shape, F32, kind="ExternalOutput").ap()
    build_program(nc, *args, result)
    r = run_bass_kernel_spmd(nc, [{f"in_{n}": a for n, a in arrays.items()}], core_ids=[0])
    return r.results[0]["out_0"]
```
